# Optimizing a Trainium2 kernel written in Bass

```python
import numpy as np
import jax
import jax.numpy as jnp

def _softmax(x, axis=-1):
    return jax.nn.softmax(x, axis=axis)

def _gelu(x):
    return jax.nn.gelu(x, approximate=True)

def _silu(x):
    return jax.nn.silu(x)

def _sigmoid(x):
    return jax.nn.sigmoid(x)

def _layernorm(x, axis=-1, eps=1e-05):
    m = jnp.mean(x, axis=axis, keepdims=True)
    v = jnp.var(x, axis=axis, keepdims=True)
    return (x - m) / jnp.sqrt(v + eps)

def _scatter_add(tgt, idx, src, axis=0):
    return tgt.at[idx].add(src)

def _segment_sum(src, seg, n):
    return jax.ops.segment_sum(src, seg, n)
kernel_name = 'mk_adaln_ffn_d2_seqx_r4_fa6ca3'

def setup_inputs(seed: int=0):
    np.random.seed(seed)
    _w = jnp.asarray

    def _rec_inputs():
        import jax
        import jax.numpy as jnp
        _rk = jax.random.key(seed)
        x = -1.394e-06 + 0.9999 * jax.random.normal(jax.random.fold_in(_rk, 1), (4, 512, 512), jnp.float32)
        _lenS = 512 - jax.random.randint(jax.random.fold_in(_rk, 7), (4,), 0, max(1, 512 // 4) + 1, jnp.int32)
        _lenS2 = 512 - jax.random.randint(jax.random.fold_in(_rk, 8), (4,), 0, max(1, 512 // 4) + 1, jnp.int32)
        cond_2048 = -0.00499425 + 1.0058 * jax.random.normal(jax.random.fold_in(_rk, 11), (4, 512), jnp.float32)
        return (x, cond_2048)
    x, cond_2048 = _rec_inputs()

    def _L0_cond_setup():
        import jax, jax.numpy as jnp
        import numpy as np
        B, T, D = (16, 128, 512)
        key = jax.random.key(seed)
        k0, k1, k2, k3 = jax.random.split(key, 4)
        scale = 1.0 / np.sqrt(D)
        return {'initial_state': jax.random.normal(k0, (B, D), jnp.float32), 'inputs': jax.random.normal(k1, (B, T, D), jnp.float32), 'W_ih': jax.random.normal(k2, (D, 3 * D), jnp.float32) * scale, 'W_hh': jax.random.normal(k3, (D, 3 * D), jnp.float32) * scale, 'b_ih': jnp.zeros((3 * D,), jnp.float32), 'b_hh': jnp.zeros((3 * D,), jnp.float32)}
    _L0_cond_all = _L0_cond_setup()
    _L0_cond_in = {k: v for k, v in _L0_cond_all.items() if k in ('W_ih', 'W_hh', 'b_ih', 'b_hh')}
    del _L0_cond_all

    def _L0_ffn_setup():
        import jax, jax.numpy as jnp
        import numpy as np
        NUM_EXPERTS = 8
        RANK = 16
        TOP_K = 2
        SCALING = 32.0 / RANK
        IN_F = 512
        OUT_F = 512
        key = jax.random.key(seed)
        k1, k2, k3, k4, k5 = jax.random.split(key, 5)
        B, T = (4, 512)
        x = jax.random.normal(k1, (B, T, IN_F), dtype=jnp.float32)
        bound_w = 1.0 / np.sqrt(IN_F)
        weight = jax.random.uniform(k2, (OUT_F, IN_F), jnp.float32, -bound_w, bound_w)
        lora_A = jax.random.uniform(k3, (NUM_EXPERTS, RANK, IN_F), jnp.float32, -bound_w, bound_w)
        lora_B = 0.02 * jax.random.normal(k4, (NUM_EXPERTS, OUT_F, RANK), dtype=jnp.float32)
        router_w = jax.random.uniform(k5, (NUM_EXPERTS, IN_F), jnp.float32, -bound_w, bound_w)
        return {'x': x, 'weight': weight, 'lora_A': lora_A, 'lora_B': lora_B, 'router_w': router_w}
    _L0_ffn_all = _L0_ffn_setup()
    _L0_ffn_in = {k: v for k, v in _L0_ffn_all.items() if k in ('weight', 'lora_A', 'lora_B', 'router_w')}
    del _L0_ffn_all

    def _L1_cond_setup():
        import jax, jax.numpy as jnp
        import numpy as np
        N, C, L_IN, L_OUT = (32, 64, 512, 512)
        key = jax.random.key(seed)
        k1, k2 = jax.random.split(key)
        inp = jax.random.normal(k1, (N, C, L_IN), dtype=jnp.float32)
        grid = jax.random.uniform(k2, (N, L_OUT), dtype=jnp.float32) * 2.0 - 1.0
        return {'input': inp, 'grid': grid, 'padding_mode': 1, 'align_corners': 1}
    _L1_cond_all = _L1_cond_setup()
    _L1_cond_in = {k: v for k, v in _L1_cond_all.items() if k in ()}
    del _L1_cond_all

    def _L1_ffn_setup():
        import jax, jax.numpy as jnp
        import numpy as np
        NUM_EXPERTS = 8
        TOP_K = 2
        key = jax.random.key(seed)
        ks = jax.random.split(key, 7)
        B, S, H, I, E = (4, 512, 512, 512, NUM_EXPERTS)
        sc = 0.02
        return {'hidden_states': jax.random.normal(ks[0], (B, S, H), dtype=jnp.float32), 'gate_w': jax.random.normal(ks[1], (E, H), dtype=jnp.float32) * sc, 'gate_b': jax.random.normal(ks[2], (E,), dtype=jnp.float32) * sc, 'w1': jax.random.normal(ks[3], (E, 2 * I, H), dtype=jnp.float32) * sc, 'b1': jax.random.normal(ks[4], (E, 2 * I), dtype=jnp.float32) * sc, 'w2': jax.random.normal(ks[5], (E, H, I), dtype=jnp.float32) * sc, 'b2': jax.random.normal(ks[6], (E, H), dtype=jnp.float32) * sc}
    _L1_ffn_all = _L1_ffn_setup()
    _L1_ffn_in = {k: v for k, v in _L1_ffn_all.items() if k in ('gate_w', 'gate_b', 'w1', 'b1', 'w2', 'b2')}
    del _L1_ffn_all
    return {'x': x, 'cond_2048': cond_2048, 'L0_cond_W_ih': _L0_cond_in['W_ih'], 'L0_cond_W_hh': _L0_cond_in['W_hh'], 'L0_cond_b_ih': _L0_cond_in['b_ih'], 'L0_cond_b_hh': _L0_cond_in['b_hh'], 'L0_ffn_weight': _L0_ffn_in['weight'], 'L0_ffn_lora_A': _L0_ffn_in['lora_A'], 'L0_ffn_lora_B': _L0_ffn_in['lora_B'], 'L0_ffn_router_w': _L0_ffn_in['router_w'], 'L1_ffn_gate_w': _L1_ffn_in['gate_w'], 'L1_ffn_gate_b': _L1_ffn_in['gate_b'], 'L1_ffn_w1': _L1_ffn_in['w1'], 'L1_ffn_b1': _L1_ffn_in['b1'], 'L1_ffn_w2': _L1_ffn_in['w2'], 'L1_ffn_b2': _L1_ffn_in['b2']}

def reference(x, cond_2048, L0_cond_W_ih, L0_cond_W_hh, L0_cond_b_ih, L0_cond_b_hh, L0_ffn_weight, L0_ffn_lora_A, L0_ffn_lora_B, L0_ffn_router_w, L1_ffn_gate_w, L1_ffn_gate_b, L1_ffn_w1, L1_ffn_b1, L1_ffn_w2, L1_ffn_b2):
    import jax
    import jax.numpy as jnp

    def _L0_cond_ref(initial_state, inputs, W_ih, W_hh, b_ih, b_hh):
        import jax, jax.numpy as jnp
        import numpy as np
        B, T, D = (16, 128, 512)
        "ScanOverTime(GRU cell): sequential per-timestep module call with\n            dict-state passing; merge_dict_trees stacks the per-step\n            'state_predicted' tensors along axis=1 -> [B, T, D]."

        def cell(h, x):
            gi = x @ W_ih + b_ih
            gh = h @ W_hh + b_hh
            i_r, i_z, i_n = jnp.split(gi, 3, axis=-1)
            h_r, h_z, h_n = jnp.split(gh, 3, axis=-1)
            r = jax.nn.sigmoid(i_r + h_r)
            z = jax.nn.sigmoid(i_z + h_z)
            n = jnp.tanh(i_n + r * h_n)
            h_new = (1.0 - z) * n + z * h
            return (h_new, h_new)
        xs = jnp.swapaxes(inputs, 0, 1)
        _, hs = jax.lax.scan(cell, initial_state, xs)
        return jnp.swapaxes(hs, 0, 1)

    def _L0_ffn_ref(x, weight, lora_A, lora_B, router_w):
        import jax, jax.numpy as jnp
        import numpy as np
        NUM_EXPERTS = 8
        RANK = 16
        TOP_K = 2
        SCALING = 32.0 / RANK
        IN_F = 512
        OUT_F = 512
        B, T, D = x.shape
        N = B * T
        base = jnp.einsum('btd,od->bto', x, weight)
        logits = jnp.einsum('btd,ed->bte', x, router_w)
        probs = jax.nn.softmax(logits, axis=-1)
        topk_vals, topk_idx = jax.lax.top_k(probs, TOP_K)
        topk_vals = topk_vals / topk_vals.sum(axis=-1, keepdims=True)
        w_dense = jnp.zeros((N, NUM_EXPERTS), dtype=x.dtype).at[jnp.arange(N)[:, None], topk_idx.reshape(N, TOP_K)].set(topk_vals.reshape(N, TOP_K))
        x_flat = x.reshape(N, D)
        Ax = jnp.einsum('nd,erd->ner', x_flat, lora_A)
        expert_out = jnp.einsum('ner,ne,eor->no', Ax, w_dense, lora_B) * SCALING
        return base + expert_out.reshape(B, T, OUT_F)

    def _L1_cond_ref(input, grid, padding_mode, align_corners):
        import jax, jax.numpy as jnp
        import numpy as np
        N, C, L_IN, L_OUT = (32, 64, 512, 512)
        L = input.shape[2]
        if align_corners:
            ix = (grid + 1.0) * 0.5 * (L - 1)
        else:
            ix = ((grid + 1.0) * L - 1.0) * 0.5
        x0 = jnp.floor(ix)
        w1 = ix - x0
        w0 = 1.0 - w1
        i0 = x0.astype(jnp.int32)
        i1 = i0 + 1
        i0c = jnp.clip(i0, 0, L - 1)
        i1c = jnp.clip(i1, 0, L - 1)
        v0 = jnp.take_along_axis(input, i0c[:, None, :], axis=2)
        v1 = jnp.take_along_axis(input, i1c[:, None, :], axis=2)
        if padding_mode:
            return w0[:, None, :] * v0 + w1[:, None, :] * v1
        else:
            m0 = ((i0 >= 0) & (i0 < L)).astype(input.dtype)
            m1 = ((i1 >= 0) & (i1 < L)).astype(input.dtype)
            return (w0 * m0)[:, None, :] * v0 + (w1 * m1)[:, None, :] * v1

    def _L1_ffn_ref(hidden_states, gate_w, gate_b, w1, b1, w2, b2):
        import jax, jax.numpy as jnp
        import numpy as np
        NUM_EXPERTS = 8
        TOP_K = 2
        B, S, H = hidden_states.shape
        x = hidden_states.reshape(-1, H)
        logits = x @ gate_w.T + gate_b
        top_vals, top_idx = jax.lax.top_k(logits, TOP_K)
        routing = jax.nn.softmax(top_vals.astype(jnp.float32), axis=-1).astype(x.dtype)
        out = jnp.zeros_like(x)
        E = w1.shape[0]
        for e in range(E):
            h = x @ w1[e].T + b1[e]
            x_glu = h[:, 0::2]
            x_lin = h[:, 1::2]
            y = x_glu * jax.nn.sigmoid(1.702 * x_glu) * (x_lin + 1.0)
            ye = y @ w2[e].T + b2[e]
            we = jnp.sum(routing * (top_idx == e), axis=-1)
            out = out + ye * we[:, None]
        return out.reshape(B, S, H)
    x = x + _L0_ffn_ref(_L0_cond_ref(cond_2048, x, L0_cond_W_ih, L0_cond_W_hh, L0_cond_b_ih, L0_cond_b_hh), L0_ffn_weight, L0_ffn_lora_A, L0_ffn_lora_B, L0_ffn_router_w)
    x = x + _L1_ffn_ref(_L1_cond_ref(x, cond_2048, 1, 1), L1_ffn_gate_w, L1_ffn_gate_b, L1_ffn_w1, L1_ffn_b1, L1_ffn_w2, L1_ffn_b2)
    return x

_drawn_inputs = setup_inputs


def setup_inputs(seed=0):
    import zlib

    import numpy as np

    out = dict(_drawn_inputs(seed))
    spreads = {'L0_cond_b_ih': (0.0, 0.1), 'L0_cond_b_hh': (0.0, 0.305)}
    factors = {'L1_ffn_gate_b': 3.988, 'L1_ffn_b1': 8.0, 'L1_ffn_b2': 4.114}
    for name, (base, spread) in spreads.items():
        noise = np.random.default_rng([zlib.crc32(name.encode()), seed]).standard_normal(out[name].shape)
        drawn = base * np.exp(spread * noise) if base else spread * noise
        out[name] = jnp.asarray(drawn.astype(out[name].dtype))
    for name, factor in factors.items():
        out[name] = (out[name] * factor).astype(out[name].dtype)
    return out
```

```python
import numpy as np
import concourse.bass as bass
from concourse import mybir
from contextlib import ExitStack

F32 = mybir.dt.float32
F16 = mybir.dt.float16
I32 = mybir.dt.int32
U32 = mybir.dt.uint32
ACT = mybir.ActivationFunctionType
ALU = mybir.AluOpType

B, T, D = 4, 512, 512
P = 128
K = D // P
TB = 64
NB = T // TB
N = B * TB
G3 = 3 * K
E = 8
RANK = 16
HALF = (K * 2 * D + K * D) // 2
HEAD = 12
ITERS = 4
STEPS = (TB - HEAD) // ITERS
CHUNK = 512
CONV = 2 * 2 * HALF // CHUNK
TT = N // P
LORA_SCALE = 32.0 / RANK

AS, WS = 16.0, 64.0
PS = AS * WS
YS = AS / (PS * PS)

LEAD = 8
FREE = LEAD - 1

ORDER = [("up", 0), ("up", 1), ("down", 0), ("up", 2), ("down", 1), ("gi", 0), ("up", 3), ("down", 2),
         ("up", 4), ("down", 3), ("gi", 1), ("up", 5), ("down", 4), ("up", 6), ("down", 5), ("up", 7),
         ("down", 6), ("gi", 2), ("down", 7)]
PARTS = ((0, 0), (1, 0), (0, 1))
UP = [(half, k, w, a) for half in range(2) for k in range(K) for w, a in PARTS]
DOWN = [(h, w, a) for h in range(K) for w, a in PARTS]
GI = [(k, w, a) for k in range(K) for w, a in PARTS]
SIZE = {"up": len(UP), "down": len(DOWN), "gi": len(GI)}


def pieces(kinds):
    flat = [(kind, i, j) for kind, i in ORDER if kind in kinds for j in range(SIZE[kind])]
    return [flat[s * len(flat) // STEPS:(s + 1) * len(flat) // STEPS] for s in range(STEPS)]


def ended(slots, kind):
    return [[i for k, i, j in slot if k == kind and j == SIZE[kind] - 1] for slot in slots]


def adaln_ffn_kernel(nc, x, h0, grid, w_ih, w_hh, b_ih, b_hh, w_base, lora_a, lora_b, w_router,
                     w_gate, b_gate, w_moe, b1, b2, ident, sel_rank, sel_all, iota_e, iota_f, out):
    scratch = nc.dram_tensor("moe_split", (2 * E, P, 2, HALF), F16).ap()
    ctx = ExitStack()
    with ctx:
        def sb(name, shape, dt):
            return ctx.enter_context(nc.sbuf_tensor(name, shape, dt))

        def pb(name):
            return ctx.enter_context(nc.psum_tensor(name, [P, 512], F32))

        def sem(name):
            return ctx.enter_context(nc.semaphore(name))

        whh = sb("whh", [P, 2, K, 3 * D], F16)
        wih = sb("wih", [P, 2, K, 3 * D], F16)
        wm = sb("wm", [P, 2, 2, 2, HALF], F16)
        wbase = sb("wbase", [P, 2, K, D], F16)
        wla = sb("wla", [P, 2, K, P], F16)
        wlb = sb("wlb", [P, 2, D], F16)
        gm = sb("gm", [P, 2, B, K, D], F16)
        wr = sb("wr", [P, K, E], F32)
        wg = sb("wg", [P, K, E], F32)
        bg16 = sb("bg16", [P, E], F32)
        idt = sb("idt", [P, P], F32)
        selr = sb("selr", [E, P], F32)
        sela = sb("sela", [E, E, P], F32)
        iote = sb("iote", [P, E], F32)
        iotf = sb("iotf", [P, 2 * K], F32)
        bi = sb("bi", [P, G3], F32)
        bh = sb("bh", [P, G3], F32)
        bn = sb("bn", [P, K, B], F32)
        b1s = sb("b1s", [P, E, 2, K], F32)
        b1sig = sb("b1sig", [P, E, K], F32)
        b2s = sb("b2s", [E, D], F32)
        gi = sb("gi", [P, G3, B, 2 * TB], F32)
        xc = sb("xc", [P, K, N], F32)
        xs = sb("xs", [P, 2, K, N], F16)
        hf = sb("hf", [P, K, B, TB], F32)
        hx = sb("hx", [P, K, N], F32)
        hxs = sb("hxs", [P, 2, K, N], F16)
        x1 = sb("x1", [P, K, N], F32)
        x1s = sb("x1s", [P, 2, K, N], F16)
        wb = sb("wb", [P, E, N], F32)
        wx = sb("wx", [P, N], F32)
        axw = sb("axw", [P, N], F32)
        axs = sb("axs", [P, 2, N], F16)
        glu = sb("glu", [P, 2, N], F32)
        lin = sb("lin", [P, 2, N], F32)
        ys = sb("ys", [P, 2, 2, N], F16)
        h = sb("h", [P, K, B], F32)
        hs = sb("hs", [P, K, 2, B], F16)
        part = sb("part", [P, 3, K, B], F32)
        pre = sb("pre", [P, 3, K, B], F32)
        rg = sb("rg", [P, K, B], F32)
        zg = sb("zg", [P, K, B], F32)
        ng = sb("ng", [P, K, B], F32)
        rn = sb("rn", [P, K, B], F32)
        na = sb("na", [P, K, B], F32)
        dh = sb("dh", [P, K, B], F32)
        zd = sb("zd", [P, K, B], F32)
        lg = sb("lg", [P, TT, E], F32)
        top = sb("top", [P, TT, E], F32)
        tix = sb("tix", [P, TT, E], U32)
        tif = sb("tif", [P, TT, 2], F32)
        tdf = sb("tdf", [P, TT, 2], F32)
        tpr = sb("tpr", [P, TT, 2], F32)
        tw = sb("tw", [P, 3, TT, E], F32)
        wt = sb("wt", [E, N], F32)
        wm32 = [wm[:, i].rearrange("p a b n -> p (a b n)").bitcast(F32) for i in range(2)]
        st_base = wb[:, :, :].rearrange("p e n -> p (e n)")
        st_la = x1[:, 0:2, :].rearrange("p k n -> p (k n)")
        st_lb = x1[:, 2:4, :].rearrange("p k n -> p (k n)")
        flat = wb[:, :, :].rearrange("p e n -> p (e n)").rearrange("p (a n) -> p a n", n=D)
        g_in, g_w1, g_i1, g_t = (flat[:, i] for i in range(4))
        flat2 = x1[:, :, :].rearrange("p k n -> p (k n)").rearrange("p (a n) -> p a n", n=D)
        g_i0, g_w0 = flat2[:, 0], flat2[:, 1]
        g_int = hx[:, 0:2, :].rearrange("p k n -> p (k n)").bitcast(I32)
        g_a = hx[:, 2:4, :].rearrange("p k n -> p (k n)")

        bank_g = [pb(f"bank_g{i}") for i in range(3)]
        bank_gi = pb("bank_gi")
        bank_acc = [pb(f"bank_acc{i}") for i in range(2)]
        bank_up = [pb(f"bank_up{i}") for i in range(2)]
        pg = [b[:, 0:K * 2 * B].rearrange("p (j s b) -> p j s b", s=2, b=B) for b in bank_g]
        p_log = bank_gi[:, 0:TT * E].rearrange("p (t e) -> p t e", e=E)
        p_wt = bank_gi[0:E, N:2 * N]

        def p_wb(e):
            if e < 4:
                return bank_up[e // 2][:, (e % 2) * N:(e % 2 + 1) * N]
            if e < 6:
                return bank_gi[:, (e - 4) * N:(e - 3) * N]
            return bank_g[1][:, (e - 6) * N:(e - 5) * N]

        names = """
            const_in bias_in wih_in whh_in l0_in x_in xres_in grid_in
            setup_dve setup_act weights_split moe_lo moe_hi
            h_ready gates_mm r_pre n_pre z_pre r_done n_done z_done gru_chain h_kept
            x_hi x_split gi_mm gi_done
            hx_copied h_hi h_lo router_mm top_diff top_prob dense_w top_chain wt_mm wt_done
            ax_mm wx_done axw_done ax_hi ax_lo l0_mm x1_done x1_hi x1_lo
            sample_mm sample_done sample_hi sample_lo wb_mm wb_act wb_dve
            up_mm sig_done act_done y_done y_hi y_lo down_mm final_done out_stored
            grid_chain grid_done
        """.split()
        S = {n: sem(n) for n in names}
        stage_in = [sem("stage_in_a"), sem("stage_in_b")]
        stored = [sem("stored_a"), sem("stored_b")]
        w_in = [sem("w_in_a"), sem("w_in_b")]

        passed = {e.engine: sem(f"passed_{n}") for n, e in (("dve", nc.vector), ("pool", nc.gpsimd))}

        block = ctx.enter_context(nc.Block())
        TOP_CHAIN = 11
        GRU_CHAIN = 8
        GRID_CHAIN = 11 + 7 * K
        OPS = GRID_CHAIN // STEPS
        assert OPS * STEPS == GRID_CHAIN
        PAIR = pieces(("up", "down", "gi"))
        PAIR_FFN = pieces(("up", "down"))
        ONLY_GI = pieces(("gi",))

        def apart(engine):
            engine.sem_inc(passed[engine.engine], 1)

        @block.sync
        def _(sp):
            sp.dma_start(wm32[0], w_ih).then_inc(S["wih_in"], 16)
            sp.dma_start(xc[:, :, :], x[0]).then_inc(S["x_in"], 16)
            for dst, src in ((bi[:, :], b_ih), (bh[:, :], b_hh), (h[:, :, :], h0),
                             (b1s[:, :, :, :], b1), (b2s[:, :], b2),
                             (bg16[:, :], b_gate.to_broadcast([P, E]))):
                sp.dma_start(dst, src).then_inc(S["bias_in"], 16)
            sp.dma_start(wm32[1], w_hh).then_inc(S["whh_in"], 16)
            for dst, src in ((st_base, w_base), (st_la, lora_a), (st_lb, lora_b)):
                sp.dma_start(dst, src).then_inc(S["l0_in"], 16)
            for dst, src in ((idt[:, :], ident), (selr[:, :], sel_rank), (sela[:, :, :], sel_all),
                             (iote[:, :], iota_e), (iotf[:, :], iota_f), (wr[:, :, :], w_router),
                             (wg[:, :, :], w_gate)):
                sp.dma_start(dst, src).then_inc(S["const_in"], 16)

            sp.wait_ge(S["x_split"], 1)
            sp.dma_start(xc[:, :, :], x[1]).then_inc(S["x_in"], 16)
            sp.wait_ge(S["weights_split"], 3)

            def load_half(n, par):
                sp.dma_start(wm32[0][:, par * HALF:(par + 1) * HALF],
                             w_moe[bass.ds(n, 1)] if not isinstance(n, int) else w_moe[n:n + 1]
                             ).then_inc(stage_in[par], 16)

            load_half(0, 0)
            load_half(1, 1)

            def pair(it, more):
                for q in range(4):
                    if q == 0:
                        sp.wait_ge(S["grid_chain"], it * GRID_CHAIN + 1)
                        sp.dma_start(g_in, grid[bass.ds(it, 1)].to_broadcast([P, D])
                                     if not isinstance(it, int) else grid[it:it + 1].to_broadcast([P, D])
                                     ).then_inc(S["grid_in"], 16)
                    n = it * 4 + q
                    sp.wait_ge(S["moe_lo"], (it * 4 + (q + 1)) * (HALF // CHUNK))
                    dst = scratch[bass.ds(n, 1)] if not isinstance(n, int) else scratch[n:n + 1]
                    sp.dma_start(dst, wm[:, 1, q % 2]).then_inc(stored[q % 2], 16)
                    if more or q < 2:
                        load_half(it * 4 + (q + 2), q % 2)

            with sp.Fori(0, ITERS - 1) as it:
                pair(it, True)
            pair(ITERS - 1, False)
            for par in range(2):
                sp.wait_ge(stored[par], 16 * E + 16)

            experts = scratch.rearrange("(e h) p l n -> e p h (l n)", h=2)

            def ffn_block(f, x_next):
                if x_next:
                    sp.dma_start(xc[:, :, :], x[bass.ds((f + 2) % NB, 1)]).then_inc(S["x_in"], 16)
                    sp.wait_ge(S["x_split"], f + 3)
                src = x[f:f + 1] if isinstance(f, int) else x[bass.ds(f, 1)]
                sp.dma_start(xc[:, :, :], src).then_inc(S["xres_in"], 16)
                def loads(it):
                    for e in range(2):
                        sp.wait_ge(S["down_mm"], f * 32 + it * 8 + K * (e + 1))
                        sp.dma_start(wm[:, e].rearrange("p h l n -> p h (l n)"),
                                     experts[bass.ds(it * 2 + e, 1)]).then_inc(w_in[e], 16)
                with sp.Fori(0, ITERS) as it:
                    loads(it)
                sp.wait_ge(S["final_done"], f * 2 + 2)
                dst = out[f:f + 1] if isinstance(f, int) else out[bass.ds(f, 1)]
                sp.dma_start(dst, x1[:, :, :]).then_inc(S["out_stored"], 16)

            with sp.Fori(0, NB - 1) as f:
                ffn_block(f, True)
            ffn_block(NB - 1, False)
            sp.wait_ge(S["out_stored"], 16 * NB + 16)

        @block.tensor
        def _(pe):
            mm = nc.tensor.matmul

            def gru(t, wb_f=None):
                pe.wait_ge(S["h_ready"], t + 1)
                for g in (0, 2, 1):
                    if g == 1 and wb_f is not None:
                        pe.wait_ge(S["wb_dve"], wb_f + 1)
                    for j in range(K):
                        col = (g * K + j) * P
                        for k in range(K):
                            for w in range(2):
                                last = mm(pg[g][:, j], whh[:, w, k, col:col + P], hs[:, k],
                                          start=(k == 0 and w == 0), stop=(k == K - 1 and w == 1))
                    last.then_inc(S["gates_mm"], 1)

            def gi_piece(m, bank, done, j):
                k, w, a = GI[j]
                if j == 0 and not (isinstance(done, int) and done <= 0):
                    pe.wait_ge(S["gi_done"], done)
                lhs = wih[:, w, k, m * P:(m + 1) * P] if isinstance(m, int) else wih[:, w, k, bass.ds(m * P, P)]
                i = mm(bank[:, 0:N], lhs, xs[:, a, k], start=(j == 0), stop=(j == len(GI) - 1))
                if j == len(GI) - 1:
                    i.then_inc(S["gi_mm"], 1)

            def up_piece(f, it, i, j):
                half, k, w, a = UP[j]
                e, tile = i // K, i % K
                if j == 0:
                    if tile == 0:
                        pe.wait_ge(w_in[e], (f * ITERS + it + 1) * 16)
                    if i == 0:
                        pe.wait_ge(S["sample_lo"], f + 1)
                        pe.wait_ge(S["wb_act"], f * 2 + 2)
                    pe.wait_ge(S["act_done"], f * 32 + it * 8 + (i + FREE))
                at = k * 2 * D + half * D + tile * P
                r = mm(bank_up[i % 2][:, half * N:(half + 1) * N],
                       wm[:, e, at // HALF, w, at % HALF:at % HALF + P], hxs[:, a, k],
                       start=(k == 0 and w == 0 and a == 0), stop=(k == K - 1 and a == 1))
                if j == len(UP) - 1:
                    r.then_inc(S["up_mm"], 1)

            def down_piece(f, it, i, j):
                hh, w, a = DOWN[j]
                e, tile = i // K, i % K
                if j == 0:
                    pe.wait_ge(S["y_lo"], f * 32 + it * 8 + (i + 1 + LEAD))
                at = K * 2 * D + tile * D + hh * P
                r = mm(bank_acc[hh // 2][:, (hh % 2) * N:(hh % 2 + 1) * N],
                       wm[:, e, at // HALF, w, at % HALF:at % HALF + P], ys[:, i % 2, a],
                       start=False, stop=False, skip_group_check=True)
                if j == len(DOWN) - 1:
                    r.then_inc(S["down_mm"], 1)

            def head(s, f, t):
                if s == 1:
                    pe.wait_ge(S["hx_copied"], f + 1)
                    for tt in range(TT):
                        for k in range(K):
                            last = mm(p_log[:, tt], hx[:, k, tt * P:(tt + 1) * P], wr[:, k], start=(k == 0), stop=(k == K - 1))
                    last.then_inc(S["router_mm"], 1)
                if s in (3, 10):
                    which = int(s == 10)
                    pe.wait_ge(S["dense_w"], f * 2 + which + 1)
                    for tt in range(TT):
                        last = mm(bank_gi[0:E, N + tt * P:N + (tt + 1) * P], tw[:, 2, tt], idt[:, :], start=True, stop=True)
                    last.then_inc(S["wt_mm"], 1)
                if s == 4:
                    pe.wait_ge(S["wt_done"], f * 2 + 1)
                    mm(bank_acc[0][:, 0:N], selr[:, :], wt[:, :], start=True, stop=True)
                    pe.wait_ge(S["h_lo"], f + 1)
                    for k in range(K):
                        for w, a in PARTS:
                            last = mm(bank_acc[0][:, N:2 * N], wla[:, w, k], hxs[:, a, k],
                                      start=(k == 0 and w == 0 and a == 0), stop=(k == K - 1 and a == 1))
                    last.then_inc(S["ax_mm"], 1)
                if s == 5:
                    pe.wait_ge(S["ax_lo"], f + 1)
                    for o in range(K):
                        dst = bank_up[o // 2][:, (o % 2) * N:(o % 2 + 1) * N]
                        for k in range(K):
                            for w, a in PARTS:
                                mm(dst, wbase[:, w, k, o * P:(o + 1) * P], hxs[:, a, k],
                                   start=(k == 0 and w == 0 and a == 0), stop=False)
                        for w, a in PARTS:
                            last = mm(dst, wlb[:, w, o * P:(o + 1) * P], axs[:, a], start=False, stop=(a == 1))
                    last.then_inc(S["l0_mm"], 1)
                if s == 7:
                    pe.wait_ge(S["x1_lo"], f + 1)
                    for l in range(K):
                        for b in range(B):
                            dst = bank_acc[l // 2][:, (l % 2) * N + b * TB:(l % 2) * N + (b + 1) * TB]
                            for k in range(K):
                                for w, a in PARTS:
                                    last = mm(dst, gm[:, w, b, k, l * P:(l + 1) * P], x1s[:, a, k, b * TB:(b + 1) * TB],
                                              start=(k == 0 and w == 0 and a == 0), stop=(k == K - 1 and a == 1))
                    last.then_inc(S["sample_mm"], 1)
                if s == 8:
                    pe.wait_ge(S["sample_done"], f + 1)
                    for tt in range(TT):
                        for k in range(K):
                            last = mm(p_log[:, tt], hx[:, k, tt * P:(tt + 1) * P], wg[:, k], start=(k == 0), stop=(k == K - 1))
                    last.then_inc(S["router_mm"], 1)
                if s == 11:
                    pe.wait_ge(S["wt_done"], f * 2 + 2)
                    for hh in range(K):
                        mm(bank_acc[hh // 2][:, (hh % 2) * N:(hh % 2 + 1) * N], b2s[:, hh * P:(hh + 1) * P], wt[:, :],
                           start=(hh % 2 == 0), stop=False, skip_group_check=True)
                    for e in range(E):
                        if e == 6 and t is not None:
                            pe.wait_ge(S["z_pre"], t + 1)
                        last = mm(p_wb(e), sela[:, e], wt[:, :], start=True, stop=True)
                    last.then_inc(S["wb_mm"], 1)

            def blk(g, gru_on, ffn_on, gi_on):
                f = g - 1
                for s in range(HEAD):
                    if gru_on:
                        gru(g * TB + s)
                    if ffn_on:
                        head(s, f, g * TB + s if gru_on else None)
                slots = PAIR if ffn_on and gi_on else PAIR_FFN if ffn_on else ONLY_GI
                with pe.Fori(0, ITERS) as it:
                    for s in range(STEPS):
                        if gru_on:
                            gru(g * TB + it * STEPS + (HEAD + s), f if ffn_on and s == 0 else None)
                        for kind, i, j in slots[s]:
                            if kind == "gi":
                                if ffn_on and i == 0 and j == 0:
                                    pe.wait_ge(S["wb_dve"], f + 1)
                                gi_piece(it * 3 + i, bank_gi, g * G3 + it * 3 + (i + G3), j)
                            if kind == "up":
                                up_piece(f, it, i, j)
                            if kind == "down":
                                down_piece(f, it, i, j)

            pe.wait_ge(S["x_split"], 1)
            pe.wait_ge(S["weights_split"], 1)
            for m in range(G3):
                for j in range(len(GI)):
                    gi_piece(m, (bank_gi, bank_acc[0])[m % 2], m - 1, j)
            pe.wait_ge(S["weights_split"], 2)
            pe.wait_ge(S["const_in"], 16 * 7)
            pe.wait_ge(S["bias_in"], 16 * 6)
            pe.wait_ge(S["setup_act"], 3)
            blk(0, True, False, True)
            pe.wait_ge(S["weights_split"], 4)
            pe.wait_ge(S["grid_done"], 1)
            with pe.Fori(1, NB) as g:
                blk(g, True, True, True)
            blk(NB, False, True, False)

        @block.scalar
        def _(act):
            def run(dst, src, func, **kw):
                return nc.scalar.activation(dst, src, func, **kw)

            def gru_r(t):
                act.wait_ge(S["r_pre"], t + 1)
                run(rg[:, :, :], pre[:, 0], ACT.Sigmoid, scale=1 / PS).then_inc(S["r_done"], 1)

            def gru_nz(t):
                act.wait_ge(S["n_pre"], t + 1)
                run(ng[:, :, :], na[:, :, :], ACT.Tanh, scale=1 / PS).then_inc(S["n_done"], 1)
                act.wait_ge(S["z_pre"], t + 1)
                run(zg[:, :, :], pre[:, 1], ACT.Sigmoid, scale=1 / PS).then_inc(S["z_done"], 1)

            def gi_out(m, bank, chunk, col):
                act.wait_ge(S["gi_mm"], chunk * G3 + (m + 1))
                src = bank[:, 0:N].rearrange("p (b t) -> p b t", t=TB)
                if isinstance(m, int) and isinstance(col, int):
                    dst, bias = gi[:, m, :, col:col + TB], bi[:, m:m + 1]
                else:
                    dst, bias = gi[:, bass.ds(m, 1), :, bass.ds(col, TB)], bi[:, bass.ds(m, 1)]
                run(dst, src, ACT.Identity, bias=bias).then_inc(S["gi_done"], 1)

            def x_hi(chunk):
                act.wait_ge(S["x_in"], (chunk + 1) * 16)
                if not isinstance(chunk, int) or chunk:
                    act.wait_ge(S["gi_mm"], chunk * G3)
                run(xs[:, 0], xc[:, :, :], ACT.Copy, scale=AS).then_inc(S["x_hi"], 1)

            def head_mid(s, f):
                if s == 5:
                    act.wait_ge(S["axw_done"], f + 1)
                    run(axs[:, 0], axw[:, :], ACT.Copy).then_inc(S["ax_hi"], 1)
                if s == 6:
                    act.wait_ge(S["x1_done"], f * 2 + 2)
                    run(x1s[:, 0], x1[:, :, :], ACT.Copy, scale=AS).then_inc(S["x1_hi"], 1)
                if s == 8:
                    act.wait_ge(S["sample_done"], f + 1)
                    run(hxs[:, 0], hx[:, :, :], ACT.Copy).then_inc(S["sample_hi"], 1)

            def head_end(s, f):
                if s == 0:
                    act.wait_ge(S["h_kept"], f * TB + TB)
                    run(hx[:, :, :], hf[:, :, :, :].rearrange("p k b t -> p k (b t)"), ACT.Copy).then_inc(S["hx_copied"], 1)
                    act.wait_ge(S["hx_copied"], f + 1)
                    act.wait_ge(S["down_mm"], f * 32 + LEAD)
                    run(hxs[:, 0], hx[:, :, :], ACT.Copy).then_inc(S["h_hi"], 1)
                if s in (1, 8):
                    which = int(s == 8)
                    act.wait_ge(S["top_diff"], f * 2 + which + 1)
                    run(tpr[:, :, :], tdf[:, :, :], ACT.Sigmoid, scale=1 / AS).then_inc(S["top_prob"], 1)
                if s in (3, 10):
                    which = int(s == 10)
                    act.wait_ge(S["wt_mm"], f * 2 + which + 1)
                    run(wt[:, :], p_wt, ACT.Copy).then_inc(S["wt_done"], 1)
                if s == 4:
                    act.wait_ge(S["ax_mm"], f + 1)
                    run(wx[:, :], bank_acc[0][:, 0:N], ACT.Copy, scale=LORA_SCALE / WS).then_inc(S["wx_done"], 1)
                if s == 7:
                    act.wait_ge(S["sample_mm"], f + 1)
                    for q in range(2):
                        i = run(hx[:, 2 * q:2 * q + 2, :].rearrange("p k n -> p (k n)"), bank_acc[q][:, :], ACT.Copy, scale=1 / WS)
                    i.then_inc(S["sample_done"], 1)
                if s == 11:
                    act.wait_ge(S["wb_mm"], f + 1)
                    for q in range(2):
                        run(wb[:, 2 * q:2 * q + 2, :].rearrange("p k n -> p (k n)"), bank_up[q][:, :], ACT.Copy,
                            scale=YS).then_inc(S["wb_act"], 1)

            def tile_mid(f, it, i):
                act.wait_ge(S["y_done"], f * 32 + it * 8 + (i + 1 + LEAD))
                act.wait_ge(S["down_mm"], f * 32 + it * 8 + (i + FREE))
                run(ys[:, i % 2, 0], lin[:, i % 2], ACT.Copy).then_inc(S["y_hi"], 1)

            def tile_end(f, it, i):
                act.wait_ge(S["up_mm"], f * 32 + it * 8 + (i + 1))
                act.wait_ge(S["y_done"], f * 32 + it * 8 + (i + FREE))
                run(glu[:, i % 2], bank_up[i % 2][:, 0:N], ACT.Sigmoid, scale=1.702 / PS,
                    bias=b1sig[:, bass.ds(it * 2 + i // K, 1), i % K]).then_inc(S["sig_done"], 1)

            def blk(g, gru_on, ffn_on, gi_on):
                f = g - 1
                for s in range(HEAD):
                    if gru_on:
                        gru_r(g * TB + s)
                    if ffn_on:
                        head_mid(s, f)
                    if gru_on:
                        gru_nz(g * TB + s)
                    if ffn_on:
                        head_end(s, f)
                    if gi_on and s == 2:
                        x_hi(g + 1)
                slots = PAIR if ffn_on and gi_on else PAIR_FFN if ffn_on else ONLY_GI
                ups, gis = ended(slots, "up"), ended(slots, "gi")
                with act.Fori(0, ITERS) as it:
                    for s in range(STEPS):
                        t = g * TB + it * STEPS + (HEAD + s)
                        if gru_on:
                            gru_r(t)
                        if ffn_on and s:
                            for i in ups[s - 1]:
                                tile_mid(f, it, i)
                        if gru_on:
                            gru_nz(t)
                        if ffn_on:
                            for i in ups[s]:
                                tile_end(f, it, i)
                        for q in gis[s]:
                            gi_out(it * 3 + q, bank_gi, g + 1, ((g + 1) % 2) * TB)
                        if not ffn_on:
                            for c in range(CONV):
                                if c * STEPS // CONV == s:
                                    moe_hi(it, c)
                    assert not ups[STEPS - 1]

            def moe_hi(it, c):
                per = HALF // CHUNK
                q = c // per
                if c % per == 0:
                    act.wait_ge(stage_in[q % 2], (it * 2 + (q // 2 + 1)) * 16)
                    act.wait_ge(stored[q % 2], (it * 2 + (q // 2 + 1)) * 16)
                at = (c % per) * CHUNK
                run(wm[:, 1, q % 2, 0, at:at + CHUNK], wm32[0][:, (q % 2) * HALF + at:(q % 2) * HALF + at + CHUNK],
                    ACT.Copy, scale=WS).then_inc(S["moe_hi"], 1)

            act.wait_ge(S["wih_in"], 16)
            wih_f = wih[:, :].rearrange("p l k n -> p l (k n)")
            whh_f = whh[:, :].rearrange("p l k n -> p l (k n)")
            run(wih_f[:, 0], wm32[0], ACT.Copy, scale=WS).then_inc(S["setup_act"], 1)
            x_hi(0)
            act.wait_ge(S["whh_in"], 16)
            run(whh_f[:, 0], wm32[1], ACT.Copy, scale=WS).then_inc(S["setup_act"], 1)
            act.wait_ge(S["bias_in"], 16 * 6)
            run(b2s[:, :], b2s[:, :], ACT.Copy, scale=PS).then_inc(S["setup_act"], 1)
            act.wait_ge(S["l0_in"], 48)
            run(wbase[:, 0].rearrange("p k n -> p (k n)"), st_base, ACT.Copy, scale=WS)
            run(wla[:, 0].rearrange("p k n -> p (k n)"), st_la, ACT.Copy, scale=WS)
            run(wlb[:, 0], st_lb, ACT.Copy, scale=WS).then_inc(S["setup_act"], 1)
            act.wait_ge(S["setup_dve"], 8)
            for m in range(G3):
                gi_out(m, (bank_gi, bank_acc[0])[m % 2], 0, 0)
            blk(0, True, False, True)
            with act.Fori(1, NB) as g:
                blk(g, True, True, True)
            blk(NB, False, True, False)

        @block.vector
        def _(dve):
            V = nc.vector
            tt_, ts_, stt_ = V.tensor_tensor, V.tensor_scalar, V.scalar_tensor_tensor

            def gru(t, base, static=False):
                n = [0]

                def link(i):
                    n[0] += 1
                    i.then_inc(S["gru_chain"], 1)
                    dve.wait_ge(S["gru_chain"], t * GRU_CHAIN + n[0])

                col = bass.ds(base, 1) if not isinstance(base, int) else slice(base, base + 1)

                def gates(g):
                    return gi[:, g * K:(g + 1) * K, :, col]

                dve.wait_ge(S["gates_mm"], t * 3 + 1)
                link(tt_(part[:, 0], pg[0][:, :, 0], gates(0), ALU.add))
                tt_(pre[:, 0], pg[0][:, :, 1], part[:, 0], ALU.add).then_inc(S["r_pre"], 1)
                dve.wait_ge(S["gates_mm"], t * 3 + 2)
                link(tt_(part[:, 2], pg[2][:, :, 0], bn[:, :, :], ALU.add))
                link(tt_(pre[:, 2], pg[2][:, :, 1], part[:, 2], ALU.add))
                dve.wait_ge(S["r_done"], t + 1)
                link(tt_(rn[:, :, :], pre[:, 2], rg[:, :, :], ALU.mult))
                tt_(na[:, :, :], rn[:, :, :], gates(2), ALU.add).then_inc(S["n_pre"], 1)
                dve.wait_ge(S["gates_mm"], t * 3 + 3)
                link(tt_(part[:, 1], pg[1][:, :, 0], gates(1), ALU.add))
                tt_(pre[:, 1], pg[1][:, :, 1], part[:, 1], ALU.add).then_inc(S["z_pre"], 1)
                dve.wait_ge(S["n_done"], t + 1)
                link(stt_(dh[:, :, :], ng[:, :, :], -AS, h[:, :, :], ALU.mult, ALU.add))
                dve.wait_ge(S["z_done"], t + 1)
                if not (isinstance(t, int) and t == 0):
                    dve.wait_ge(S["h_kept"], t)
                link(tt_(zd[:, :, :], dh[:, :, :], zg[:, :, :], ALU.mult))
                stt_(hs[:, :, 0], ng[:, :, :], AS, zd[:, :, :], ALU.mult, ALU.add)
                link(stt_(h[:, :, :], ng[:, :, :], AS, zd[:, :, :], ALU.mult, ALU.add))
                tt_(hs[:, :, 1], h[:, :, :], hs[:, :, 0], ALU.subtract).then_inc(S["h_ready"], 1)
                assert n[0] == GRU_CHAIN, n

            def x_lo(chunk):
                dve.wait_ge(S["x_hi"], chunk + 1)
                stt_(xs[:, 1], xc[:, :, :], AS, xs[:, 0], ALU.mult, ALU.subtract).then_inc(S["x_split"], 1)

            def top_a(which, f):
                n = [0]
                base = (f * 2 + which) * TOP_CHAIN

                def link(i):
                    n[0] += 1
                    i.then_inc(S["top_chain"], 1)
                    dve.wait_ge(S["top_chain"], base + n[0])

                dve.wait_ge(S["router_mm"], f * 2 + which + 1)
                if which:
                    link(tt_(lg[:, :, :], p_log, bg16[:, :].unsqueeze(1).to_broadcast([P, TT, E]), ALU.add))
                else:
                    link(V.tensor_copy(lg[:, :, :], p_log))
                for tt in range(TT):
                    apart(dve)
                    link(V.max(top[:, tt], lg[:, tt]))
                for tt in range(TT):
                    apart(dve)
                    link(V.max_index(tix[:, tt], top[:, tt], lg[:, tt]))
                link(V.tensor_copy(tif[:, :, :], tix[:, :, 0:2]))
                link(tt_(tdf[:, :, 0:1], top[:, :, 0:1], top[:, :, 1:2], ALU.subtract))
                tt_(tdf[:, :, 1:2], top[:, :, 1:2], top[:, :, 0:1], ALU.subtract).then_inc(S["top_diff"], 1)
                assert n[0] == 7

            def top_b(which, f):
                n = [7]
                base = (f * 2 + which) * TOP_CHAIN

                def link(i):
                    n[0] += 1
                    i.then_inc(S["top_chain"], 1)
                    dve.wait_ge(S["top_chain"], base + n[0])

                dve.wait_ge(S["top_prob"], f * 2 + which + 1)
                for tt in range(TT):
                    for c in range(2):
                        link(ts_(tw[:, c, tt], iote[:, :], tif[:, tt, c:c + 1], tpr[:, tt, c:c + 1], ALU.is_equal, ALU.mult))
                tt_(tw[:, 2], tw[:, 0], tw[:, 1], ALU.add).then_inc(S["dense_w"], 1)
                assert n[0] == TOP_CHAIN

            def head(s, f):
                if s == 0:
                    dve.wait_ge(S["h_hi"], f + 1)
                    tt_(hxs[:, 1], hx[:, :, :], hxs[:, 0], ALU.subtract).then_inc(S["h_lo"], 1)
                if s in (1, 8):
                    top_a(int(s == 8), f)
                if s in (2, 9):
                    top_b(int(s == 9), f)
                if s == 4:
                    dve.wait_ge(S["wx_done"], f + 1)
                    tt_(axw[:, :], bank_acc[0][:, N:2 * N], wx[:, :], ALU.mult).then_inc(S["axw_done"], 1)
                if s == 5:
                    dve.wait_ge(S["l0_mm"], f + 1)
                    dve.wait_ge(S["xres_in"], f * 16 + 16)
                    dve.wait_ge(S["out_stored"], f * 16 + 16)
                    for q in range(2):
                        sl = slice(2 * q, 2 * q + 2)
                        stt_(x1[:, sl, :].rearrange("p k n -> p (k n)"), bank_up[q][:, :], 1 / PS,
                             xc[:, sl, :].rearrange("p k n -> p (k n)"), ALU.mult, ALU.add).then_inc(S["x1_done"], 1)
                if s == 6:
                    dve.wait_ge(S["x1_hi"], f + 1)
                    stt_(x1s[:, 1], x1[:, :, :], AS, x1s[:, 0], ALU.mult, ALU.subtract).then_inc(S["x1_lo"], 1)
                if s == 10:
                    dve.wait_ge(S["sample_hi"], f + 1)
                    tt_(hxs[:, 1], hx[:, :, :], hxs[:, 0], ALU.subtract).then_inc(S["sample_lo"], 1)
                if s == 11:
                    dve.wait_ge(S["wb_mm"], f + 1)
                    ts_(wb[:, 4:6, :].rearrange("p k n -> p (k n)"), bank_gi[:, :], YS, None, ALU.mult)
                    ts_(wb[:, 6:8, :].rearrange("p k n -> p (k n)"), bank_g[1][:, :], YS, None,
                        ALU.mult).then_inc(S["wb_dve"], 1)

            def tile(f, it, i):
                e = it * 2 + i // K
                dve.wait_ge(S["up_mm"], f * 32 + it * 8 + (i + 1))
                dve.wait_ge(S["y_lo"], f * 32 + it * 8 + (i + FREE))
                if i == 0:
                    dve.wait_ge(S["wb_act"], f * 2 + 2)
                    dve.wait_ge(S["wb_dve"], f + 1)
                dve.wait_ge(S["sig_done"], f * 32 + it * 8 + (i + 1))
                stt_(lin[:, i % 2], bank_up[i % 2][:, N:2 * N], b1s[:, bass.ds(e, 1), 1, i % K],
                     wb[:, bass.ds(e, 1)], ALU.add, ALU.mult)
                stt_(glu[:, i % 2], bank_up[i % 2][:, 0:N], b1s[:, bass.ds(e, 1), 0, i % K],
                     glu[:, i % 2], ALU.add, ALU.mult).then_inc(S["act_done"], 1)

            def moe_lo(it, c):
                per = HALF // CHUNK
                q = c // per
                at = (c % per) * CHUNK
                dve.wait_ge(S["moe_hi"], it * CONV + (c + 1))
                stt_(wm[:, 1, q % 2, 1, at:at + CHUNK], wm32[0][:, (q % 2) * HALF + at:(q % 2) * HALF + at + CHUNK],
                     WS, wm[:, 1, q % 2, 0, at:at + CHUNK], ALU.mult, ALU.subtract).then_inc(S["moe_lo"], 1)

            def blk(g, gru_on, ffn_on, gi_on):
                f = g - 1
                if gru_on:
                    dve.wait_ge(S["gi_done"], g * G3 + G3)
                for s in range(HEAD):
                    if gru_on:
                        gru(g * TB + s, (g % 2) * TB + s)
                    if ffn_on:
                        head(s, f)
                    if gi_on and s == 3:
                        x_lo(g + 1)
                slots = PAIR if ffn_on and gi_on else PAIR_FFN if ffn_on else ONLY_GI
                ups = ended(slots, "up")
                with dve.Fori(0, ITERS) as it:
                    for s in range(STEPS):
                        if gru_on:
                            gru(g * TB + it * STEPS + (HEAD + s), (g % 2) * TB + it * STEPS + (HEAD + s))
                        if ffn_on:
                            for i in ups[s]:
                                tile(f, it, i)
                        else:
                            for c in range(CONV):
                                if c * STEPS // CONV == s:
                                    moe_lo(it, c)
                if ffn_on:
                    dve.wait_ge(S["down_mm"], f * 32 + (32 + LEAD))
                    for q in range(2):
                        v = x1[:, 2 * q:2 * q + 2, :].rearrange("p k n -> p (k n)")
                        stt_(v, bank_acc[q][:, :], 1 / PS, v, ALU.mult, ALU.add).then_inc(S["final_done"], 1)

            n = [0]

            def step(i):
                n[0] += 1
                i.then_inc(S["setup_dve"], 1)
                dve.wait_ge(S["setup_dve"], n[0])

            wih_f = wih[:, :].rearrange("p l k n -> p l (k n)")
            whh_f = whh[:, :].rearrange("p l k n -> p l (k n)")
            dve.wait_ge(S["bias_in"], 16 * 6)
            step(tt_(bi[:, 0:2 * K], bi[:, 0:2 * K], bh[:, 0:2 * K], ALU.add))
            step(ts_(bi[:, :], bi[:, :], PS, None, ALU.mult))
            step(ts_(bn[:, :, :], bh[:, 2 * K:3 * K].unsqueeze(2).to_broadcast([P, K, B]), PS, None, ALU.mult))
            step(ts_(b1sig[:, :, :], b1s[:, :, 0], 1.702, None, ALU.mult))
            step(ts_(b1s[:, :, 1], b1s[:, :, 1], 1.0, None, ALU.add))
            step(ts_(b1s[:, :, :, :], b1s[:, :, :, :], PS, None, ALU.mult))
            step(ts_(bg16[:, :], bg16[:, :], AS, None, ALU.mult))
            step(ts_(h[:, :, :], h[:, :, :], AS, None, ALU.mult))
            dve.wait_ge(S["setup_act"], 1)
            stt_(wih_f[:, 1], wm32[0], WS, wih_f[:, 0], ALU.mult, ALU.subtract).then_inc(S["weights_split"], 1)
            x_lo(0)
            dve.wait_ge(S["setup_act"], 2)
            stt_(whh_f[:, 1], wm32[1], WS, whh_f[:, 0], ALU.mult, ALU.subtract).then_inc(S["weights_split"], 1)
            step(V.tensor_copy(hs[:, :, 0], h[:, :, :]))
            tt_(hs[:, :, 1], h[:, :, :], hs[:, :, 0], ALU.subtract).then_inc(S["h_ready"], 1)
            dve.wait_ge(S["setup_act"], 4)
            stt_(wbase[:, 1].rearrange("p k n -> p (k n)"), st_base, WS, wbase[:, 0].rearrange("p k n -> p (k n)"),
                 ALU.mult, ALU.subtract)
            stt_(wla[:, 1].rearrange("p k n -> p (k n)"), st_la, WS, wla[:, 0].rearrange("p k n -> p (k n)"),
                 ALU.mult, ALU.subtract).then_inc(S["weights_split"], 1)
            stt_(wlb[:, 1], st_lb, WS, wlb[:, 0], ALU.mult, ALU.subtract).then_inc(S["weights_split"], 1)
            dve.wait_ge(S["const_in"], 16 * 7)
            blk(0, True, False, True)
            with dve.Fori(1, NB) as g:
                blk(g, True, True, True)
            blk(NB, False, True, False)

        @block.gpsimd
        def _(pool):
            Q = nc.gpsimd

            def keep(t, col):
                pool.wait_ge(S["h_ready"], t + 2)
                apart(pool)
                dst = hf[:, :, :, col:col + 1] if isinstance(col, int) else hf[:, :, :, bass.ds(col, 1)]
                Q.tensor_copy(dst, h[:, :, :]).then_inc(S["h_kept"], 1)

            def grid_op(j, it):
                b = it * GRID_CHAIN + 1
                if j == 0:
                    pool.wait_ge(S["grid_in"], it * 16 + 16)
                else:
                    pool.wait_ge(S["grid_chain"], b + j)
                apart(pool)
                ts, tt, cp = Q.tensor_scalar, Q.tensor_tensor, Q.tensor_copy
                if j == 0:
                    i = ts(g_t, g_in, 1.0, 0.5 * (D - 1), ALU.add, ALU.mult)
                elif j == 1:
                    i = cp(g_int, g_t)
                elif j == 2:
                    i = cp(g_i0, g_int)
                elif j == 3:
                    i = tt(g_w1, g_i0, g_t, ALU.subtract)
                elif j == 4:
                    i = ts(g_w1, g_w1, 0.0, None, ALU.is_gt)
                elif j == 5:
                    i = tt(g_i0, g_i0, g_w1, ALU.subtract)
                elif j == 6:
                    i = tt(g_w1, g_t, g_i0, ALU.subtract)
                elif j == 7:
                    i = ts(g_w0, g_w1, -WS, WS, ALU.mult, ALU.add)
                elif j == 8:
                    i = ts(g_w1, g_w1, WS, None, ALU.mult)
                elif j == 9:
                    i = ts(g_i1, g_i0, -1.0, float(D - 2), ALU.max, ALU.min)
                elif j == 10:
                    i = ts(g_i0, g_i0, 0.0, float(D - 1), ALU.max, ALU.min)
                else:
                    k, o = (j - 11) // 7, (j - 11) % 7
                    hi, lo = gm[:, 0, bass.ds(it, 1), k], gm[:, 1, bass.ds(it, 1), k]
                    if o == 0:
                        i = ts(g_a, g_i0, iotf[:, k:k + 1], None, ALU.is_equal)
                    elif o == 1:
                        i = tt(g_a, g_a, g_w0, ALU.mult)
                    elif o == 2:
                        i = ts(g_t, g_i1, iotf[:, K + k:K + k + 1], None, ALU.is_equal)
                    elif o == 3:
                        i = tt(g_t, g_t, g_w1, ALU.mult)
                    elif o == 4:
                        i = tt(g_a, g_a, g_t, ALU.add)
                    elif o == 5:
                        i = cp(hi, g_a)
                    else:
                        i = tt(lo, g_a, hi, ALU.subtract)
                i.then_inc(S["grid_chain"], 1)

            def tile_y(f, it, i):
                pool.wait_ge(S["act_done"], f * 32 + it * 8 + (i + 1 + LEAD))
                Q.tensor_tensor(lin[:, i % 2], glu[:, i % 2], lin[:, i % 2], ALU.mult).then_inc(S["y_done"], 1)
                pool.wait_ge(S["y_hi"], f * 32 + it * 8 + (i + 1))
                Q.tensor_tensor(ys[:, i % 2, 1], lin[:, i % 2], ys[:, i % 2, 0], ALU.subtract).then_inc(S["y_lo"], 1)

            def blk(g, gru_on, ffn_on, gi_on):
                f = g - 1
                for s in range(HEAD):
                    if ffn_on and s == 0:
                        pool.wait_ge(S["hx_copied"], f + 1)
                    if gru_on:
                        keep(g * TB + s, s)
                    if ffn_on and s == 4:
                        pool.wait_ge(S["ax_hi"], f + 1)
                        Q.tensor_tensor(axs[:, 1], axw[:, :], axs[:, 0], ALU.subtract).then_inc(S["ax_lo"], 1)
                slots = PAIR if ffn_on and gi_on else PAIR_FFN if ffn_on else ONLY_GI
                ups = ended(slots, "up")
                with pool.Fori(0, ITERS) as it:
                    for s in range(STEPS):
                        if gru_on:
                            keep(g * TB + it * STEPS + (HEAD + s), it * STEPS + (HEAD + s))
                        if ffn_on:
                            for i in ups[s]:
                                tile_y(f, it, i)
                        else:
                            for j in range(s * OPS, (s + 1) * OPS):
                                grid_op(j, it)

            for n in ("act_done", "y_done", "y_lo", "down_mm"):
                Q.sem_inc(S[n], LEAD)
            Q.sem_inc(S["grid_chain"], 1)
            Q.sem_inc(S["out_stored"], 16)
            for s in stored:
                Q.sem_inc(s, 16)
            pool.wait_ge(S["const_in"], 16 * 7)
            pool.wait_ge(S["weights_split"], 4)
            blk(0, True, False, True)
            pool.wait_ge(S["grid_chain"], ITERS * GRID_CHAIN + 1)
            Q.tensor_copy(g_a[:, 0:1], g_a[:, 1:2]).then_inc(S["grid_done"], 1)
            with pool.Fori(1, NB) as g:
                blk(g, True, True, True)
            blk(NB, False, True, False)


def kernel(**inputs):
    import numpy as _np
    import concourse.bacc as _bacc
    from concourse import mybir as _mybir
    from concourse.bass_utils import run_bass_kernel_spmd as _run

    a = {k: _np.asarray(v) for k, v in inputs.items()}
    eye = _np.eye(P, dtype=_np.float32)

    def rows(w):
        return w.reshape(-1, P, w.shape[-1]).transpose(1, 0, 2)

    w1 = a["L1_ffn_w1"].reshape(E, D, 2, D).transpose(0, 3, 2, 1)
    w1 = w1.reshape(E, K, P, 2 * D).transpose(0, 2, 1, 3).reshape(E, P, 2 * K * D)
    w2 = a["L1_ffn_w2"].transpose(0, 2, 1).reshape(E, K, P, D).transpose(0, 2, 1, 3).reshape(E, P, K * D)
    moe = _np.concatenate([w1, w2], axis=2).reshape(E, P, 2, HALF).transpose(0, 2, 1, 3).reshape(2 * E, P, HALF)
    b1 = a["L1_ffn_b1"].reshape(E, K, P, 2).transpose(2, 0, 3, 1)
    arrays = {
        "x": a["x"].reshape(B, NB, TB, K, P).transpose(1, 4, 3, 0, 2).reshape(NB, P, K, N),
        "h0": a["cond_2048"].reshape(B, K, P).transpose(2, 1, 0),
        "grid": a["cond_2048"],
        "w_ih": rows(a["L0_cond_W_ih"]).reshape(P, -1),
        "w_hh": rows(a["L0_cond_W_hh"]).reshape(P, -1),
        "b_ih": a["L0_cond_b_ih"].reshape(G3, P).T,
        "b_hh": a["L0_cond_b_hh"].reshape(G3, P).T,
        "w_base": rows(a["L0_ffn_weight"].T).reshape(P, -1),
        "lora_a": rows(a["L0_ffn_lora_A"].reshape(E * RANK, D).T).reshape(P, -1),
        "lora_b": a["L0_ffn_lora_B"].transpose(0, 2, 1).reshape(E * RANK, D),
        "w_router": rows(a["L0_ffn_router_w"].T),
        "w_gate": rows(a["L1_ffn_gate_w"].T),
        "b_gate": a["L1_ffn_gate_b"].reshape(1, E),
        "w_moe": moe,
        "b1": b1,
        "b2": a["L1_ffn_b2"],
        "ident": eye,
        "sel_rank": _np.repeat(eye[:E, :E], RANK, axis=1),
        "sel_all": _np.repeat(eye[:E, :E], P, axis=1).reshape(E, E, P),
        "iota_e": _np.broadcast_to(_np.arange(E, dtype=_np.float32), (P, E)),
        "iota_f": (_np.arange(2 * D, dtype=_np.float32) % D - _np.repeat([0, 1], D)).astype(_np.float32).reshape(2 * K, P).T,
    }
    arrays = {k: _np.ascontiguousarray(v) for k, v in arrays.items()}
    nc = _bacc.Bacc("TRN2", target_bir_lowering=False, num_devices=1, dynamic_dma_scratch_size=2048)
    args = [nc.dram_tensor(f"in_{k}", v.shape, _mybir.dt.from_np(v.dtype), kind="ExternalInput").ap()
            for k, v in arrays.items()]
    out = nc.dram_tensor("out", (NB, P, K, N), F32, kind="ExternalOutput").ap()
    adaln_ffn_kernel(nc, *args, out)
    r = _run(nc, [{f"in_{k}": v for k, v in arrays.items()}], core_ids=[0])
    got = _np.asarray(r.results[0]["out"])
    return _np.ascontiguousarray(got.reshape(NB, P, K, B, TB).transpose(3, 0, 4, 2, 1).reshape(B, T, D))
```

```python
import numpy as np
import concourse.bass as bass
from concourse import mybir
from contextlib import ExitStack

F32 = mybir.dt.float32
F16 = mybir.dt.float16
I32 = mybir.dt.int32
U32 = mybir.dt.uint32
ACT = mybir.ActivationFunctionType
ALU = mybir.AluOpType

B, T, D = 4, 512, 512
P = 128
K = D // P
TB = 64
NB = T // TB
N = B * TB
G3 = 3 * K
E = 8
RANK = 16
HALF = (K * 2 * D + K * D) // 2
HEAD = 12
ITERS = 4
STEPS = (TB - HEAD) // ITERS
CHUNK = 512
CONV = 2 * 2 * HALF // CHUNK
TT = N // P
LORA_SCALE = 32.0 / RANK

AS, WS = 16.0, 64.0
PS = AS * WS
YS = AS / (PS * PS)

LEAD = 8
FREE = LEAD - 1

ORDER = [("up", 0), ("up", 1), ("down", 0), ("up", 2), ("down", 1), ("up", 3), ("down", 2), ("gi", 0),
         ("up", 4), ("down", 3), ("up", 5), ("down", 4), ("up", 6), ("down", 5), ("up", 7),
         ("down", 6), ("gi", 1), ("down", 7)]
GI_PAIR = 2
GI_HEAD = {5: (0, 1), 9: (2, 3)}
PARTS = ((0, 0), (1, 0), (0, 1))
UP = [(half, k, w, a) for half in range(2) for k in range(K) for w, a in PARTS]
DOWN = [(h, w, a) for h in range(K) for w, a in PARTS]
GI = [(k, w, a) for k in range(K) for w, a in PARTS]
BASE = [(o, k, w, a) for o in range(K) for k in range(K) for w, a in PARTS]
SIZE = {"up": len(UP), "down": len(DOWN), "gi": len(GI)}


def pieces(kinds):
    flat = [(kind, i, j) for kind, i in ORDER if kind in kinds for j in range(SIZE[kind])]
    return [flat[s * len(flat) // STEPS:(s + 1) * len(flat) // STEPS] for s in range(STEPS)]


def ended(slots, kind):
    return [[i for k, i, j in slot if k == kind and j == SIZE[kind] - 1] for slot in slots]


def adaln_ffn_kernel(nc, x, h0, grid, w_ih, w_hh, b_ih, b_hh, w_base, lora_a, lora_b, w_router,
                     w_gate, b_gate, w_moe, b1, b2, ident, sel_all, iota_e, iota_f, out):
    scratch = nc.dram_tensor("moe_split", (2 * E, P, 2, HALF), F16).ap()
    ctx = ExitStack()
    with ctx:
        def sb(name, shape, dt):
            return ctx.enter_context(nc.sbuf_tensor(name, shape, dt))

        def pb(name):
            return ctx.enter_context(nc.psum_tensor(name, [P, 512], F32))

        def sem(name):
            return ctx.enter_context(nc.semaphore(name))

        whh = sb("whh", [P, 2, K, 3 * D], F16)
        wih = sb("wih", [P, 2, K, 3 * D], F16)
        wm = sb("wm", [P, 2, 2, 2, HALF], F16)
        wbase = sb("wbase", [P, 2, K, D], F16)
        wla = sb("wla", [P, 2, K, P], F16)
        wlb = sb("wlb", [P, 2, D], F16)
        gm = sb("gm", [P, 2, B, K, D], F16)
        wr = sb("wr", [P, K, E], F32)
        wg = sb("wg", [P, K, E], F32)
        bg16 = sb("bg16", [P, E], F32)
        idt = sb("idt", [P, P], F32)
        sela = sb("sela", [E, E, P], F16)
        iote = sb("iote", [P, E], F32)
        iotf = sb("iotf", [P, 2 * K], F32)
        bi = sb("bi", [P, G3], F32)
        bh = sb("bh", [P, G3], F32)
        bn = sb("bn", [P, K, B], F32)
        b1s = sb("b1s", [P, E, 2, K], F32)
        b1sig = sb("b1sig", [P, E, K], F32)
        b2s = sb("b2s", [E, 2, D], F16)
        gi = sb("gi", [P, G3, B, 2 * TB], F32)
        xc = sb("xc", [P, K, N], F32)
        xr = sb("xr", [P, K, N], F32)
        xs = sb("xs", [P, 2, K, N], F16)
        hf = sb("hf", [P, K, B, TB], F32)
        hx = sb("hx", [P, K, N], F32)
        hxs = sb("hxs", [P, 2, K, N], F16)
        x1 = sb("x1", [P, K, N], F32)
        x1s = sb("x1s", [P, 2, K, N], F16)
        wb = sb("wb", [P, E, N], F32)
        axw = sb("axw", [P, TT, E, RANK], F32)
        axs = sb("axs", [P, 2, N], F16)
        glu = sb("glu", [P, 2, N], F32)
        lin = sb("lin", [P, 2, N], F32)
        ys = sb("ys", [P, 2, 2, N], F16)
        h = sb("h", [P, K, B], F32)
        hs = sb("hs", [P, K, 2, B], F16)
        part = sb("part", [P, 3, K, B], F32)
        pre = sb("pre", [P, 3, K, B], F32)
        rg = sb("rg", [P, K, B], F32)
        zg = sb("zg", [P, K, B], F32)
        ng = sb("ng", [P, K, B], F32)
        rn = sb("rn", [P, K, B], F32)
        na = sb("na", [P, K, B], F32)
        dh = sb("dh", [P, K, B], F32)
        zd = sb("zd", [P, K, B], F32)
        lg = sb("lg", [P, TT, E], F32)
        top = sb("top", [P, TT, E], F32)
        tix = sb("tix", [P, TT, E], U32)
        tif = sb("tif", [P, TT, 2], F32)
        tdf = sb("tdf", [P, TT, 2], F32)
        tpr = sb("tpr", [P, TT, 2], F32)
        tw = sb("tw", [P, 3, TT, E], F32)
        wt = sb("wt", [E, 2, N], F16)
        sela32 = hf[0:E].rearrange("p k b t -> p (k b t)").rearrange("p (e n) -> p e n", n=P)
        b2f = hx[0:E, 0:2, :].rearrange("p k n -> p (k n)")
        wm32 = [wm[:, i].rearrange("p a b n -> p (a b n)").bitcast(F32) for i in range(2)]
        st_base = wb[:, :, :].rearrange("p e n -> p (e n)")
        st_la = x1[:, 0:2, :].rearrange("p k n -> p (k n)")
        st_lb = x1[:, 2:4, :].rearrange("p k n -> p (k n)")
        flat = wb[:, :, :].rearrange("p e n -> p (e n)").rearrange("p (a n) -> p a n", n=D)
        g_in, g_w1, g_i1, g_t = (flat[:, i] for i in range(4))
        flat2 = x1[:, :, :].rearrange("p k n -> p (k n)").rearrange("p (a n) -> p a n", n=D)
        g_i0, g_w0 = flat2[:, 0], flat2[:, 1]
        g_int = hx[:, 0:2, :].rearrange("p k n -> p (k n)").bitcast(I32)
        g_a = hx[:, 2:4, :].rearrange("p k n -> p (k n)")

        bank_g = [pb(f"bank_g{i}") for i in range(3)]
        bank_gi = pb("bank_gi")
        bank_acc = [pb(f"bank_acc{i}") for i in range(2)]
        bank_up = [pb(f"bank_up{i}") for i in range(2)]
        pg = [b[:, 0:K * 2 * B].rearrange("p (j s b) -> p j s b", s=2, b=B) for b in bank_g]
        p_log = bank_gi[:, 0:TT * E].rearrange("p (t e) -> p t e", e=E)
        p_wt = bank_acc[0][0:E, 0:N]
        p_ax = bank_acc[0][:, 0:N].rearrange("p (t e r) -> p t e r", e=E, r=RANK)
        gi_bank = (bank_gi, bank_acc[1])

        def p_wb(e):
            if e < 4:
                return bank_up[e // 2][:, (e % 2) * N:(e % 2 + 1) * N]
            if e < 6:
                return bank_gi[:, (e - 4) * N:(e - 3) * N]
            return bank_g[1][:, (e - 6) * N:(e - 5) * N]

        names = """
            const_in bias_in wih_in whh_in l0_in x_in xres_in grid_in
            setup_dve setup_act weights_split moe_lo moe_hi
            h_ready gates_mm r_pre n_pre z_pre r_done n_done z_done gru_chain h_kept
            x_hi x_split gi_mm gi_done
            hx_copied h_hi h_lo router_mm top_diff top_prob dense_w top_chain
            axw_done axt_mm ax_hi ax_lo l0_mm x1_done x1_hi x1_lo
            sample_mm sample_done sample_hi sample_lo wt_mm wt_hi wt_lo wb_mm wb_act wb_dve
            up_mm sig_done act_done y_done y_hi y_lo down_mm final_done out_stored
            grid_chain grid_done
        """.split()
        S = {n: sem(n) for n in names}
        stage_in = [sem("stage_in_a"), sem("stage_in_b")]
        stored = [sem("stored_a"), sem("stored_b")]
        w_in = [sem("w_in_a"), sem("w_in_b")]

        passed = {e.engine: sem(f"passed_{n}") for n, e in (("dve", nc.vector), ("pool", nc.gpsimd))}

        block = ctx.enter_context(nc.Block())
        TOP_CHAIN = 11
        GRU_CHAIN = 8
        GRID_CHAIN = 11 + 7 * K
        OPS = GRID_CHAIN // STEPS
        assert OPS * STEPS == GRID_CHAIN
        GI0 = sum(len(tiles) for tiles in GI_HEAD.values())
        assert GI0 + ITERS * GI_PAIR == G3
        PAIR = pieces(("up", "down", "gi"))
        PAIR_FFN = pieces(("up", "down"))
        ONLY_GI = pieces(("gi",))

        def apart(engine):
            engine.sem_inc(passed[engine.engine], 1)

        @block.sync
        def _(sp):
            sp.dma_start(wm32[0], w_ih).then_inc(S["wih_in"], 16)
            sp.dma_start(xc[:, :, :], x[0]).then_inc(S["x_in"], 16)
            for dst, src in ((bi[:, :], b_ih), (bh[:, :], b_hh), (h[:, :, :], h0),
                             (b1s[:, :, :, :], b1), (b2f, b2),
                             (bg16[:, :], b_gate.to_broadcast([P, E]))):
                sp.dma_start(dst, src).then_inc(S["bias_in"], 16)
            sp.dma_start(wm32[1], w_hh).then_inc(S["whh_in"], 16)
            for dst, src in ((st_base, w_base), (st_la, lora_a), (st_lb, lora_b)):
                sp.dma_start(dst, src).then_inc(S["l0_in"], 16)
            for dst, src in ((idt[:, :], ident), (sela32[:, :, :], sel_all),
                             (iote[:, :], iota_e), (iotf[:, :], iota_f), (wr[:, :, :], w_router),
                             (wg[:, :, :], w_gate)):
                sp.dma_start(dst, src).then_inc(S["const_in"], 16)

            sp.wait_ge(S["x_split"], 1)
            sp.dma_start(xc[:, :, :], x[1]).then_inc(S["x_in"], 16)
            sp.wait_ge(S["weights_split"], 3)

            def load_half(n, par):
                sp.dma_start(wm32[0][:, par * HALF:(par + 1) * HALF],
                             w_moe[bass.ds(n, 1)] if not isinstance(n, int) else w_moe[n:n + 1]
                             ).then_inc(stage_in[par], 16)

            load_half(0, 0)
            load_half(1, 1)

            def pair(it, more):
                for q in range(4):
                    if q == 0:
                        sp.wait_ge(S["grid_chain"], it * GRID_CHAIN + 1)
                        sp.dma_start(g_in, grid[bass.ds(it, 1)].to_broadcast([P, D])
                                     if not isinstance(it, int) else grid[it:it + 1].to_broadcast([P, D])
                                     ).then_inc(S["grid_in"], 16)
                    n = it * 4 + q
                    sp.wait_ge(S["moe_lo"], (it * 4 + (q + 1)) * (HALF // CHUNK))
                    dst = scratch[bass.ds(n, 1)] if not isinstance(n, int) else scratch[n:n + 1]
                    sp.dma_start(dst, wm[:, 1, q % 2]).then_inc(stored[q % 2], 16)
                    if more or q < 2:
                        load_half(it * 4 + (q + 2), q % 2)

            with sp.Fori(0, ITERS - 1) as it:
                pair(it, True)
            pair(ITERS - 1, False)
            for par in range(2):
                sp.wait_ge(stored[par], 16 * E + 16)

            experts = scratch.rearrange("(e h) p l n -> e p h (l n)", h=2)

            def ffn_block(f, x_next):
                src = x[f:f + 1] if isinstance(f, int) else x[bass.ds(f, 1)]
                sp.dma_start(xr[:, :, :], src).then_inc(S["xres_in"], 16)
                if x_next:
                    sp.wait_ge(S["x_split"], f + 2)
                    sp.dma_start(xc[:, :, :], x[bass.ds(f + 2, 1)]).then_inc(S["x_in"], 16)
                def loads(it):
                    for e in range(2):
                        sp.wait_ge(S["down_mm"], f * 32 + it * 8 + K * (e + 1))
                        sp.dma_start(wm[:, e].rearrange("p h l n -> p h (l n)"),
                                     experts[bass.ds(it * 2 + e, 1)]).then_inc(w_in[e], 16)
                with sp.Fori(0, ITERS) as it:
                    loads(it)
                sp.wait_ge(S["final_done"], f * 2 + 2)
                dst = out[f:f + 1] if isinstance(f, int) else out[bass.ds(f, 1)]
                sp.dma_start(dst, x1[:, :, :]).then_inc(S["out_stored"], 16)

            with sp.Fori(0, NB - 2) as f:
                ffn_block(f, True)
            for f in (NB - 2, NB - 1):
                ffn_block(f, False)
            sp.wait_ge(S["out_stored"], 16 * NB + 16)

        @block.tensor
        def _(pe):
            mm = nc.tensor.matmul

            def gru(t, wb_f=None):
                pe.wait_ge(S["h_ready"], t + 1)
                for g in (0, 2, 1):
                    if g == 1 and wb_f is not None:
                        pe.wait_ge(S["wb_dve"], wb_f + 1)
                    for j in range(K):
                        col = (g * K + j) * P
                        for k in range(K):
                            for w in range(2):
                                last = mm(pg[g][:, j], whh[:, w, k, col:col + P], hs[:, k],
                                          start=(k == 0 and w == 0), stop=(k == K - 1 and w == 1))
                    last.then_inc(S["gates_mm"], 1)

            def gi_piece(m, bank, done, j):
                k, w, a = GI[j]
                if j == 0 and not (isinstance(done, int) and done <= 0):
                    pe.wait_ge(S["gi_done"], done)
                lhs = wih[:, w, k, m * P:(m + 1) * P] if isinstance(m, int) else wih[:, w, k, bass.ds(m * P, P)]
                i = mm(bank[:, 0:N], lhs, xs[:, a, k], start=(j == 0), stop=(j == len(GI) - 1))
                if j == len(GI) - 1:
                    i.then_inc(S["gi_mm"], 1)

            def up_piece(f, it, i, j):
                half, k, w, a = UP[j]
                e, tile = i // K, i % K
                if j == 0:
                    if tile == 0:
                        pe.wait_ge(w_in[e], (f * ITERS + it + 1) * 16)
                    if i == 0:
                        pe.wait_ge(S["sample_lo"], f + 1)
                        pe.wait_ge(S["wb_act"], f * 2 + 2)
                    pe.wait_ge(S["act_done"], f * 32 + it * 8 + (i + FREE))
                at = k * 2 * D + half * D + tile * P
                r = mm(bank_up[i % 2][:, half * N:(half + 1) * N],
                       wm[:, e, at // HALF, w, at % HALF:at % HALF + P], hxs[:, a, k],
                       start=(k == 0 and w == 0 and a == 0), stop=(k == K - 1 and a == 1))
                if j == len(UP) - 1:
                    r.then_inc(S["up_mm"], 1)

            def down_piece(f, it, i, j):
                hh, w, a = DOWN[j]
                e, tile = i // K, i % K
                if j == 0:
                    pe.wait_ge(S["y_lo"], f * 32 + it * 8 + (i + 1 + LEAD))
                at = K * 2 * D + tile * D + hh * P
                r = mm(bank_acc[hh // 2][:, (hh % 2) * N:(hh % 2 + 1) * N],
                       wm[:, e, at // HALF, w, at % HALF:at % HALF + P], ys[:, i % 2, a],
                       start=False, stop=False, skip_group_check=True)
                if j == len(DOWN) - 1:
                    r.then_inc(S["down_mm"], 1)

            def base(f, first, last_):
                if first == 0:
                    pe.wait_ge(S["h_lo"], f + 1)
                for o, k, w, a in BASE[first:last_]:
                    mm(bank_up[o // 2][:, (o % 2) * N:(o % 2 + 1) * N], wbase[:, w, k, o * P:(o + 1) * P], hxs[:, a, k],
                       start=(o % 2 == 0 and k == 0 and w == 0 and a == 0), stop=False, skip_group_check=True)

            def sample(first, last_):
                for l in range(first, last_):
                    for b in range(B):
                        dst = bank_acc[l // 2][:, (l % 2) * N + b * TB:(l % 2) * N + (b + 1) * TB]
                        for k in range(K):
                            for w, a in PARTS:
                                i = mm(dst, gm[:, w, b, k, l * P:(l + 1) * P], x1s[:, a, k, b * TB:(b + 1) * TB],
                                       start=(k == 0 and w == 0 and a == 0), stop=(k == K - 1 and a == 1))
                i.then_inc(S["sample_mm"], 1)

            def logits(w):
                for tt in range(TT):
                    for k in range(K):
                        i = mm(p_log[:, tt], hx[:, k, tt * P:(tt + 1) * P], w[:, k], start=(k == 0), stop=(k == K - 1))
                i.then_inc(S["router_mm"], 1)

            def head(s, f, t):
                if s == 1:
                    pe.wait_ge(S["hx_copied"], f + 1)
                    pe.wait_ge(S["h_lo"], f + 1)
                    for tt in range(TT):
                        for k in range(K):
                            for w, a in PARTS:
                                mm(bank_acc[0][:, tt * P:(tt + 1) * P], hxs[:, a, k, tt * P:(tt + 1) * P], wla[:, w, k],
                                   start=(k == 0 and w == 0 and a == 0), stop=(k == K - 1 and a == 1))
                    logits(wr)
                if s == 2:
                    base(f, 0, 24)
                if s == 3:
                    pe.wait_ge(S["axw_done"], f + 1)
                    for tt in range(TT):
                        i = mm(bank_acc[1][:, tt * P:(tt + 1) * P], axw[:, tt].rearrange("p e r -> p (e r)"), idt[:, :],
                               start=True, stop=True)
                    i.then_inc(S["axt_mm"], 1)
                    base(f, 24, 40)
                if s == 4:
                    base(f, 40, len(BASE))
                    pe.wait_ge(S["ax_lo"], f + 1)
                    for o in range(K):
                        for w, a in PARTS:
                            i = mm(bank_up[o // 2][:, (o % 2) * N:(o % 2 + 1) * N], wlb[:, w, o * P:(o + 1) * P], axs[:, a],
                                   start=False, stop=(a == 1), skip_group_check=True)
                    i.then_inc(S["l0_mm"], 1)
                if s == 6:
                    pe.wait_ge(S["x1_lo"], f + 1)
                    sample(0, 2)
                if s == 7:
                    sample(2, 4)
                if s == 8:
                    pe.wait_ge(S["sample_done"], f * 2 + 2)
                    logits(wg)
                if s == 10:
                    pe.wait_ge(S["dense_w"], f * 2 + 2)
                    for tt in range(TT):
                        i = mm(p_wt[:, tt * P:(tt + 1) * P], tw[:, 2, tt], idt[:, :], start=True, stop=True)
                    i.then_inc(S["wt_mm"], 1)
                if s == 11:
                    pe.wait_ge(S["wt_lo"], f + 1)
                    for e in range(E):
                        if e == 6 and t is not None:
                            pe.wait_ge(S["z_pre"], t + 1)
                        for a in range(2):
                            i = mm(p_wb(e), sela[:, e], wt[:, a], start=(a == 0), stop=(a == 1))
                    i.then_inc(S["wb_mm"], 1)
                    for hh in range(K):
                        for w, a in PARTS:
                            mm(bank_acc[hh // 2][:, (hh % 2) * N:(hh % 2 + 1) * N], b2s[:, w, hh * P:(hh + 1) * P], wt[:, a],
                               start=(hh % 2 == 0 and w == 0 and a == 0), stop=False, skip_group_check=True)

            def blk(g, gru_on, ffn_on, gi_on):
                f = g - 1
                for s in range(HEAD):
                    if gru_on:
                        gru(g * TB + s)
                    if ffn_on:
                        head(s, f, g * TB + s if gru_on else None)
                    if gi_on and s in GI_HEAD:
                        if s == 5:
                            pe.wait_ge(S["x_split"], g + 2)
                        if s == 5 and ffn_on:
                            pe.wait_ge(S["ax_lo"], f + 1)
                        if s == 9 and ffn_on:
                            pe.wait_ge(S["top_diff"], f * 2 + 2)
                            pe.wait_ge(S["sample_done"], f * 2 + 2)
                        for q, m in enumerate(GI_HEAD[s]):
                            for j in range(len(GI)):
                                gi_piece(m, gi_bank[q], g * G3 + (m + G3 - q), j)
                slots = PAIR if ffn_on and gi_on else PAIR_FFN if ffn_on else ONLY_GI
                with pe.Fori(0, ITERS) as it:
                    for s in range(STEPS):
                        if gru_on:
                            gru(g * TB + it * STEPS + (HEAD + s), f if ffn_on and s == 0 else None)
                        for kind, i, j in slots[s]:
                            if kind == "gi":
                                if ffn_on and i == 0 and j == 0:
                                    pe.wait_ge(S["wb_dve"], f + 1)
                                gi_piece(it * GI_PAIR + (GI0 + i), bank_gi, g * G3 + it * GI_PAIR + (G3 + GI0 + i), j)
                            if kind == "up":
                                up_piece(f, it, i, j)
                            if kind == "down":
                                down_piece(f, it, i, j)

            pe.wait_ge(S["x_split"], 1)
            pe.wait_ge(S["weights_split"], 1)
            for m in range(G3):
                for j in range(len(GI)):
                    gi_piece(m, (bank_gi, bank_acc[0])[m % 2], m - 1, j)
            pe.wait_ge(S["weights_split"], 2)
            pe.wait_ge(S["const_in"], 16 * 6)
            pe.wait_ge(S["bias_in"], 16 * 6)
            blk(0, True, False, True)
            pe.wait_ge(S["weights_split"], 4)
            pe.wait_ge(S["grid_done"], 1)
            with pe.Fori(1, NB - 1) as g:
                blk(g, True, True, True)
            blk(NB - 1, True, True, False)
            blk(NB, False, True, False)

        @block.scalar
        def _(act):
            def run(dst, src, func, **kw):
                return nc.scalar.activation(dst, src, func, **kw)

            def gru_r(t):
                act.wait_ge(S["r_pre"], t + 1)
                run(rg[:, :, :], pre[:, 0], ACT.Sigmoid, scale=1 / PS).then_inc(S["r_done"], 1)

            def gru_nz(t):
                act.wait_ge(S["n_pre"], t + 1)
                run(ng[:, :, :], na[:, :, :], ACT.Tanh, scale=1 / PS).then_inc(S["n_done"], 1)
                act.wait_ge(S["z_pre"], t + 1)
                run(zg[:, :, :], pre[:, 1], ACT.Sigmoid, scale=1 / PS).then_inc(S["z_done"], 1)

            def gi_out(m, bank, chunk, col):
                act.wait_ge(S["gi_mm"], chunk * G3 + (m + 1))
                src = bank[:, 0:N].rearrange("p (b t) -> p b t", t=TB)
                dst = gi[:, m:m + 1] if isinstance(m, int) else gi[:, bass.ds(m, 1)]
                dst = dst[:, :, :, col:col + TB] if isinstance(col, int) else dst[:, :, :, bass.ds(col, TB)]
                bias = bi[:, m:m + 1] if isinstance(m, int) else bi[:, bass.ds(m, 1)]
                run(dst, src, ACT.Identity, bias=bias).then_inc(S["gi_done"], 1)

            def x_hi(chunk):
                act.wait_ge(S["x_in"], (chunk + 1) * 16)
                if not isinstance(chunk, int) or chunk:
                    act.wait_ge(S["gi_mm"], chunk * G3)
                run(xs[:, 0], xc[:, :, :], ACT.Copy, scale=AS).then_inc(S["x_hi"], 1)

            def head_mid(s, f):
                if s == 5:
                    act.wait_ge(S["x1_done"], f * 2 + 2)
                    run(x1s[:, 0], x1[:, :, :], ACT.Copy, scale=AS).then_inc(S["x1_hi"], 1)
                if s == 9:
                    run(hxs[:, 0], hx[:, :, :], ACT.Copy).then_inc(S["sample_hi"], 1)

            def head_end(s, f):
                if s == 0:
                    act.wait_ge(S["h_kept"], f * TB + TB)
                    run(hx[:, :, :], hf[:, :, :, :].rearrange("p k b t -> p k (b t)"), ACT.Copy).then_inc(S["hx_copied"], 1)
                    act.wait_ge(S["hx_copied"], f + 1)
                    act.wait_ge(S["down_mm"], f * 32 + LEAD)
                    run(hxs[:, 0], hx[:, :, :], ACT.Copy).then_inc(S["h_hi"], 1)
                if s in (1, 8):
                    which = int(s == 8)
                    act.wait_ge(S["top_diff"], f * 2 + which + 1)
                    run(tpr[:, :, :], tdf[:, :, :], ACT.Sigmoid, scale=1 / AS).then_inc(S["top_prob"], 1)
                if s == 3:
                    act.wait_ge(S["axt_mm"], f + 1)
                    run(axs[:, 0], bank_acc[1][:, 0:N], ACT.Copy, scale=LORA_SCALE / WS).then_inc(S["ax_hi"], 1)
                if s in (6, 7):
                    q = s - 6
                    act.wait_ge(S["sample_mm"], f * 2 + (q + 1))
                    run(hx[:, 2 * q:2 * q + 2, :].rearrange("p k n -> p (k n)"), bank_acc[q][:, :], ACT.Copy,
                        scale=1 / WS).then_inc(S["sample_done"], 1)
                if s == 10:
                    act.wait_ge(S["wt_mm"], f + 1)
                    run(wt[:, 0], p_wt, ACT.Copy, scale=AS).then_inc(S["wt_hi"], 1)
                if s == 11:
                    act.wait_ge(S["wb_mm"], f + 1)
                    for q in range(2):
                        run(wb[:, 2 * q:2 * q + 2, :].rearrange("p k n -> p (k n)"), bank_up[q][:, :], ACT.Copy,
                            scale=YS / AS).then_inc(S["wb_act"], 1)

            def tile_mid(f, it, i):
                act.wait_ge(S["y_done"], f * 32 + it * 8 + (i + 1 + LEAD))
                act.wait_ge(S["down_mm"], f * 32 + it * 8 + (i + FREE))
                run(ys[:, i % 2, 0], lin[:, i % 2], ACT.Copy).then_inc(S["y_hi"], 1)

            def tile_end(f, it, i):
                act.wait_ge(S["up_mm"], f * 32 + it * 8 + (i + 1))
                act.wait_ge(S["y_done"], f * 32 + it * 8 + (i + FREE))
                run(glu[:, i % 2], bank_up[i % 2][:, 0:N], ACT.Sigmoid, scale=1.702 / PS,
                    bias=b1sig[:, bass.ds(it * 2 + i // K, 1), i % K]).then_inc(S["sig_done"], 1)

            def blk(g, gru_on, ffn_on, gi_on):
                f = g - 1
                for s in range(HEAD):
                    if gru_on:
                        gru_r(g * TB + s)
                    if ffn_on:
                        head_mid(s, f)
                    if gru_on:
                        gru_nz(g * TB + s)
                    if ffn_on:
                        head_end(s, f)
                    if gi_on and s == 2:
                        x_hi(g + 1)
                    if gi_on and s in GI_HEAD:
                        for q, m in enumerate(GI_HEAD[s]):
                            gi_out(m, gi_bank[q], g + 1, ((g + 1) % 2) * TB)
                slots = PAIR if ffn_on and gi_on else PAIR_FFN if ffn_on else ONLY_GI
                ups, gis = ended(slots, "up"), ended(slots, "gi")
                with act.Fori(0, ITERS) as it:
                    for s in range(STEPS):
                        t = g * TB + it * STEPS + (HEAD + s)
                        if gru_on:
                            gru_r(t)
                        if ffn_on and s:
                            for i in ups[s - 1]:
                                tile_mid(f, it, i)
                        if gru_on:
                            gru_nz(t)
                        if ffn_on:
                            for i in ups[s]:
                                tile_end(f, it, i)
                        for q in gis[s]:
                            gi_out(it * GI_PAIR + (GI0 + q), bank_gi, g + 1, ((g + 1) % 2) * TB)
                        if not ffn_on:
                            for c in range(CONV):
                                if c * STEPS // CONV == s:
                                    moe_hi(it, c)
                    assert not ups[STEPS - 1]

            def moe_hi(it, c):
                per = HALF // CHUNK
                q = c // per
                if c % per == 0:
                    act.wait_ge(stage_in[q % 2], (it * 2 + (q // 2 + 1)) * 16)
                    act.wait_ge(stored[q % 2], (it * 2 + (q // 2 + 1)) * 16)
                at = (c % per) * CHUNK
                run(wm[:, 1, q % 2, 0, at:at + CHUNK], wm32[0][:, (q % 2) * HALF + at:(q % 2) * HALF + at + CHUNK],
                    ACT.Copy, scale=WS).then_inc(S["moe_hi"], 1)

            act.wait_ge(S["wih_in"], 16)
            wih_f = wih[:, :].rearrange("p l k n -> p l (k n)")
            whh_f = whh[:, :].rearrange("p l k n -> p l (k n)")
            run(wih_f[:, 0], wm32[0], ACT.Copy, scale=WS).then_inc(S["setup_act"], 1)
            x_hi(0)
            act.wait_ge(S["whh_in"], 16)
            run(whh_f[:, 0], wm32[1], ACT.Copy, scale=WS).then_inc(S["setup_act"], 1)
            act.wait_ge(S["bias_in"], 16 * 6)
            run(b2s[:, 0], b2f, ACT.Copy, scale=WS).then_inc(S["setup_act"], 1)
            act.wait_ge(S["const_in"], 16 * 6)
            run(sela[:, :, :], sela32[:, :, :], ACT.Copy)
            act.wait_ge(S["l0_in"], 48)
            run(wbase[:, 0].rearrange("p k n -> p (k n)"), st_base, ACT.Copy, scale=WS)
            run(wla[:, 0].rearrange("p k n -> p (k n)"), st_la, ACT.Copy, scale=WS)
            run(wlb[:, 0], st_lb, ACT.Copy, scale=WS).then_inc(S["setup_act"], 1)
            act.wait_ge(S["setup_dve"], 8)
            for m in range(G3):
                gi_out(m, (bank_gi, bank_acc[0])[m % 2], 0, 0)
            blk(0, True, False, True)
            with act.Fori(1, NB - 1) as g:
                blk(g, True, True, True)
            blk(NB - 1, True, True, False)
            blk(NB, False, True, False)

        @block.vector
        def _(dve):
            V = nc.vector
            tt_, ts_, stt_ = V.tensor_tensor, V.tensor_scalar, V.scalar_tensor_tensor

            def gru(t, base, static=False):
                n = [0]

                def link(i):
                    n[0] += 1
                    i.then_inc(S["gru_chain"], 1)
                    dve.wait_ge(S["gru_chain"], t * GRU_CHAIN + n[0])

                col = bass.ds(base, 1) if not isinstance(base, int) else slice(base, base + 1)

                def gates(g):
                    return gi[:, g * K:(g + 1) * K, :, col]

                dve.wait_ge(S["gates_mm"], t * 3 + 1)
                link(tt_(part[:, 0], pg[0][:, :, 0], gates(0), ALU.add))
                tt_(pre[:, 0], pg[0][:, :, 1], part[:, 0], ALU.add).then_inc(S["r_pre"], 1)
                dve.wait_ge(S["gates_mm"], t * 3 + 2)
                link(tt_(part[:, 2], pg[2][:, :, 0], bn[:, :, :], ALU.add))
                link(tt_(pre[:, 2], pg[2][:, :, 1], part[:, 2], ALU.add))
                dve.wait_ge(S["r_done"], t + 1)
                link(tt_(rn[:, :, :], pre[:, 2], rg[:, :, :], ALU.mult))
                tt_(na[:, :, :], rn[:, :, :], gates(2), ALU.add).then_inc(S["n_pre"], 1)
                dve.wait_ge(S["gates_mm"], t * 3 + 3)
                link(tt_(part[:, 1], pg[1][:, :, 0], gates(1), ALU.add))
                tt_(pre[:, 1], pg[1][:, :, 1], part[:, 1], ALU.add).then_inc(S["z_pre"], 1)
                dve.wait_ge(S["n_done"], t + 1)
                link(stt_(dh[:, :, :], ng[:, :, :], -AS, h[:, :, :], ALU.mult, ALU.add))
                dve.wait_ge(S["z_done"], t + 1)
                if not (isinstance(t, int) and t == 0):
                    dve.wait_ge(S["h_kept"], t)
                link(tt_(zd[:, :, :], dh[:, :, :], zg[:, :, :], ALU.mult))
                stt_(hs[:, :, 0], ng[:, :, :], AS, zd[:, :, :], ALU.mult, ALU.add)
                link(stt_(h[:, :, :], ng[:, :, :], AS, zd[:, :, :], ALU.mult, ALU.add))
                tt_(hs[:, :, 1], h[:, :, :], hs[:, :, 0], ALU.subtract).then_inc(S["h_ready"], 1)
                assert n[0] == GRU_CHAIN, n

            def x_lo(chunk):
                dve.wait_ge(S["x_hi"], chunk + 1)
                stt_(xs[:, 1], xc[:, :, :], AS, xs[:, 0], ALU.mult, ALU.subtract).then_inc(S["x_split"], 1)

            def top_a(which, f):
                n = [0]
                base = (f * 2 + which) * TOP_CHAIN

                def link(i):
                    n[0] += 1
                    i.then_inc(S["top_chain"], 1)
                    dve.wait_ge(S["top_chain"], base + n[0])

                dve.wait_ge(S["router_mm"], f * 2 + which + 1)
                if which:
                    link(tt_(lg[:, :, :], p_log, bg16[:, :].unsqueeze(1).to_broadcast([P, TT, E]), ALU.add))
                else:
                    link(V.tensor_copy(lg[:, :, :], p_log))
                for tt in range(TT):
                    apart(dve)
                    link(V.max(top[:, tt], lg[:, tt]))
                for tt in range(TT):
                    apart(dve)
                    link(V.max_index(tix[:, tt], top[:, tt], lg[:, tt]))
                link(V.tensor_copy(tif[:, :, :], tix[:, :, 0:2]))
                link(tt_(tdf[:, :, 0:1], top[:, :, 0:1], top[:, :, 1:2], ALU.subtract))
                tt_(tdf[:, :, 1:2], top[:, :, 1:2], top[:, :, 0:1], ALU.subtract).then_inc(S["top_diff"], 1)
                assert n[0] == 7

            def top_b(which, f):
                n = [7]
                base = (f * 2 + which) * TOP_CHAIN

                def link(i):
                    n[0] += 1
                    i.then_inc(S["top_chain"], 1)
                    dve.wait_ge(S["top_chain"], base + n[0])

                dve.wait_ge(S["top_prob"], f * 2 + which + 1)
                for tt in range(TT):
                    for c in range(2):
                        link(ts_(tw[:, c, tt], iote[:, :], tif[:, tt, c:c + 1], tpr[:, tt, c:c + 1], ALU.is_equal, ALU.mult))
                tt_(tw[:, 2], tw[:, 0], tw[:, 1], ALU.add).then_inc(S["dense_w"], 1)
                if not which:
                    dve.wait_ge(S["dense_w"], f * 2 + 1)
                    tt_(axw[:, :, :, :], p_ax, tw[:, 2].unsqueeze(3).to_broadcast([P, TT, E, RANK]),
                        ALU.mult).then_inc(S["axw_done"], 1)
                assert n[0] == TOP_CHAIN

            def head(s, f):
                if s == 0:
                    dve.wait_ge(S["h_hi"], f + 1)
                    tt_(hxs[:, 1], hx[:, :, :], hxs[:, 0], ALU.subtract).then_inc(S["h_lo"], 1)
                if s in (1, 8):
                    top_a(int(s == 8), f)
                if s in (2, 9):
                    top_b(int(s == 9), f)
                if s == 3:
                    dve.wait_ge(S["ax_hi"], f + 1)
                    stt_(axs[:, 1], bank_acc[1][:, 0:N], LORA_SCALE / WS, axs[:, 0], ALU.mult, ALU.subtract).then_inc(S["ax_lo"], 1)
                if s == 4:
                    dve.wait_ge(S["l0_mm"], f + 1)
                    dve.wait_ge(S["xres_in"], f * 16 + 16)
                    dve.wait_ge(S["out_stored"], f * 16 + 16)
                    for q in range(2):
                        sl = slice(2 * q, 2 * q + 2)
                        stt_(x1[:, sl, :].rearrange("p k n -> p (k n)"), bank_up[q][:, :], 1 / PS,
                             xr[:, sl, :].rearrange("p k n -> p (k n)"), ALU.mult, ALU.add).then_inc(S["x1_done"], 1)
                if s == 5:
                    dve.wait_ge(S["x1_hi"], f + 1)
                    stt_(x1s[:, 1], x1[:, :, :], AS, x1s[:, 0], ALU.mult, ALU.subtract).then_inc(S["x1_lo"], 1)
                if s == 10:
                    dve.wait_ge(S["wt_hi"], f + 1)
                    stt_(wt[:, 1], p_wt, AS, wt[:, 0], ALU.mult, ALU.subtract).then_inc(S["wt_lo"], 1)
                    dve.wait_ge(S["sample_hi"], f + 1)
                    tt_(hxs[:, 1], hx[:, :, :], hxs[:, 0], ALU.subtract).then_inc(S["sample_lo"], 1)
                if s == 11:
                    dve.wait_ge(S["wb_mm"], f + 1)
                    ts_(wb[:, 4:6, :].rearrange("p k n -> p (k n)"), bank_gi[:, :], YS / AS, None, ALU.mult)
                    ts_(wb[:, 6:8, :].rearrange("p k n -> p (k n)"), bank_g[1][:, :], YS / AS, None,
                        ALU.mult).then_inc(S["wb_dve"], 1)

            def tile(f, it, i):
                e = it * 2 + i // K
                dve.wait_ge(S["up_mm"], f * 32 + it * 8 + (i + 1))
                dve.wait_ge(S["y_lo"], f * 32 + it * 8 + (i + FREE))
                if i == 0:
                    dve.wait_ge(S["wb_act"], f * 2 + 2)
                    dve.wait_ge(S["wb_dve"], f + 1)
                dve.wait_ge(S["sig_done"], f * 32 + it * 8 + (i + 1))
                stt_(lin[:, i % 2], bank_up[i % 2][:, N:2 * N], b1s[:, bass.ds(e, 1), 1, i % K],
                     wb[:, bass.ds(e, 1)], ALU.add, ALU.mult)
                stt_(glu[:, i % 2], bank_up[i % 2][:, 0:N], b1s[:, bass.ds(e, 1), 0, i % K],
                     glu[:, i % 2], ALU.add, ALU.mult).then_inc(S["act_done"], 1)

            def moe_lo(it, c):
                per = HALF // CHUNK
                q = c // per
                at = (c % per) * CHUNK
                dve.wait_ge(S["moe_hi"], it * CONV + (c + 1))
                stt_(wm[:, 1, q % 2, 1, at:at + CHUNK], wm32[0][:, (q % 2) * HALF + at:(q % 2) * HALF + at + CHUNK],
                     WS, wm[:, 1, q % 2, 0, at:at + CHUNK], ALU.mult, ALU.subtract).then_inc(S["moe_lo"], 1)

            def blk(g, gru_on, ffn_on, gi_on):
                f = g - 1
                if gru_on:
                    dve.wait_ge(S["gi_done"], g * G3 + G3)
                for s in range(HEAD):
                    if gru_on:
                        gru(g * TB + s, (g % 2) * TB + s)
                    if ffn_on:
                        head(s, f)
                    if gi_on and s == 3:
                        x_lo(g + 1)
                slots = PAIR if ffn_on and gi_on else PAIR_FFN if ffn_on else ONLY_GI
                ups = ended(slots, "up")
                with dve.Fori(0, ITERS) as it:
                    for s in range(STEPS):
                        if gru_on:
                            gru(g * TB + it * STEPS + (HEAD + s), (g % 2) * TB + it * STEPS + (HEAD + s))
                        if ffn_on:
                            for i in ups[s]:
                                tile(f, it, i)
                        else:
                            for c in range(CONV):
                                if c * STEPS // CONV == s:
                                    moe_lo(it, c)
                if ffn_on:
                    dve.wait_ge(S["down_mm"], f * 32 + (32 + LEAD))
                    for q in range(2):
                        v = x1[:, 2 * q:2 * q + 2, :].rearrange("p k n -> p (k n)")
                        stt_(v, bank_acc[q][:, :], 1 / PS, v, ALU.mult, ALU.add).then_inc(S["final_done"], 1)

            n = [0]

            def step(i):
                n[0] += 1
                i.then_inc(S["setup_dve"], 1)
                dve.wait_ge(S["setup_dve"], n[0])

            wih_f = wih[:, :].rearrange("p l k n -> p l (k n)")
            whh_f = whh[:, :].rearrange("p l k n -> p l (k n)")
            dve.wait_ge(S["bias_in"], 16 * 6)
            step(tt_(bi[:, 0:2 * K], bi[:, 0:2 * K], bh[:, 0:2 * K], ALU.add))
            step(ts_(bi[:, :], bi[:, :], PS, None, ALU.mult))
            step(ts_(bn[:, :, :], bh[:, 2 * K:3 * K].unsqueeze(2).to_broadcast([P, K, B]), PS, None, ALU.mult))
            step(ts_(b1sig[:, :, :], b1s[:, :, 0], 1.702, None, ALU.mult))
            step(ts_(b1s[:, :, 1], b1s[:, :, 1], 1.0, None, ALU.add))
            step(ts_(b1s[:, :, :, :], b1s[:, :, :, :], PS, None, ALU.mult))
            step(ts_(bg16[:, :], bg16[:, :], AS, None, ALU.mult))
            step(ts_(h[:, :, :], h[:, :, :], AS, None, ALU.mult))
            dve.wait_ge(S["setup_act"], 1)
            stt_(wih_f[:, 1], wm32[0], WS, wih_f[:, 0], ALU.mult, ALU.subtract).then_inc(S["weights_split"], 1)
            x_lo(0)
            dve.wait_ge(S["setup_act"], 2)
            stt_(whh_f[:, 1], wm32[1], WS, whh_f[:, 0], ALU.mult, ALU.subtract).then_inc(S["weights_split"], 1)
            step(V.tensor_copy(hs[:, :, 0], h[:, :, :]))
            dve.wait_ge(S["setup_act"], 3)
            stt_(b2s[:, 1], b2f, WS, b2s[:, 0], ALU.mult, ALU.subtract)
            tt_(hs[:, :, 1], h[:, :, :], hs[:, :, 0], ALU.subtract).then_inc(S["h_ready"], 1)
            dve.wait_ge(S["setup_act"], 4)
            stt_(wbase[:, 1].rearrange("p k n -> p (k n)"), st_base, WS, wbase[:, 0].rearrange("p k n -> p (k n)"),
                 ALU.mult, ALU.subtract)
            stt_(wla[:, 1].rearrange("p k n -> p (k n)"), st_la, WS, wla[:, 0].rearrange("p k n -> p (k n)"),
                 ALU.mult, ALU.subtract).then_inc(S["weights_split"], 1)
            stt_(wlb[:, 1], st_lb, WS, wlb[:, 0], ALU.mult, ALU.subtract).then_inc(S["weights_split"], 1)
            dve.wait_ge(S["const_in"], 16 * 6)
            blk(0, True, False, True)
            with dve.Fori(1, NB - 1) as g:
                blk(g, True, True, True)
            blk(NB - 1, True, True, False)
            blk(NB, False, True, False)

        @block.gpsimd
        def _(pool):
            Q = nc.gpsimd

            def keep(t, col):
                pool.wait_ge(S["h_ready"], t + 2)
                apart(pool)
                dst = hf[:, :, :, col:col + 1] if isinstance(col, int) else hf[:, :, :, bass.ds(col, 1)]
                Q.tensor_copy(dst, h[:, :, :]).then_inc(S["h_kept"], 1)

            def grid_op(j, it):
                b = it * GRID_CHAIN + 1
                if j == 0:
                    pool.wait_ge(S["grid_in"], it * 16 + 16)
                else:
                    pool.wait_ge(S["grid_chain"], b + j)
                apart(pool)
                ts, tt, cp = Q.tensor_scalar, Q.tensor_tensor, Q.tensor_copy
                if j == 0:
                    i = ts(g_t, g_in, 1.0, 0.5 * (D - 1), ALU.add, ALU.mult)
                elif j == 1:
                    i = cp(g_int, g_t)
                elif j == 2:
                    i = cp(g_i0, g_int)
                elif j == 3:
                    i = tt(g_w1, g_i0, g_t, ALU.subtract)
                elif j == 4:
                    i = ts(g_w1, g_w1, 0.0, None, ALU.is_gt)
                elif j == 5:
                    i = tt(g_i0, g_i0, g_w1, ALU.subtract)
                elif j == 6:
                    i = tt(g_w1, g_t, g_i0, ALU.subtract)
                elif j == 7:
                    i = ts(g_w0, g_w1, -WS, WS, ALU.mult, ALU.add)
                elif j == 8:
                    i = ts(g_w1, g_w1, WS, None, ALU.mult)
                elif j == 9:
                    i = ts(g_i1, g_i0, -1.0, float(D - 2), ALU.max, ALU.min)
                elif j == 10:
                    i = ts(g_i0, g_i0, 0.0, float(D - 1), ALU.max, ALU.min)
                else:
                    k, o = (j - 11) // 7, (j - 11) % 7
                    hi, lo = gm[:, 0, bass.ds(it, 1), k], gm[:, 1, bass.ds(it, 1), k]
                    if o == 0:
                        i = ts(g_a, g_i0, iotf[:, k:k + 1], None, ALU.is_equal)
                    elif o == 1:
                        i = tt(g_a, g_a, g_w0, ALU.mult)
                    elif o == 2:
                        i = ts(g_t, g_i1, iotf[:, K + k:K + k + 1], None, ALU.is_equal)
                    elif o == 3:
                        i = tt(g_t, g_t, g_w1, ALU.mult)
                    elif o == 4:
                        i = tt(g_a, g_a, g_t, ALU.add)
                    elif o == 5:
                        i = cp(hi, g_a)
                    else:
                        i = tt(lo, g_a, hi, ALU.subtract)
                i.then_inc(S["grid_chain"], 1)

            def tile_y(f, it, i):
                pool.wait_ge(S["act_done"], f * 32 + it * 8 + (i + 1 + LEAD))
                Q.tensor_tensor(lin[:, i % 2], glu[:, i % 2], lin[:, i % 2], ALU.mult).then_inc(S["y_done"], 1)
                pool.wait_ge(S["y_hi"], f * 32 + it * 8 + (i + 1))
                Q.tensor_tensor(ys[:, i % 2, 1], lin[:, i % 2], ys[:, i % 2, 0], ALU.subtract).then_inc(S["y_lo"], 1)

            def blk(g, gru_on, ffn_on, gi_on):
                f = g - 1
                for s in range(HEAD):
                    if ffn_on and s == 0:
                        pool.wait_ge(S["hx_copied"], f + 1)
                    if gru_on:
                        keep(g * TB + s, s)
                slots = PAIR if ffn_on and gi_on else PAIR_FFN if ffn_on else ONLY_GI
                ups = ended(slots, "up")
                with pool.Fori(0, ITERS) as it:
                    for s in range(STEPS):
                        if gru_on:
                            keep(g * TB + it * STEPS + (HEAD + s), it * STEPS + (HEAD + s))
                        if ffn_on:
                            for i in ups[s]:
                                tile_y(f, it, i)
                        else:
                            for j in range(s * OPS, (s + 1) * OPS):
                                grid_op(j, it)

            for n in ("act_done", "y_done", "y_lo", "down_mm"):
                Q.sem_inc(S[n], LEAD)
            Q.sem_inc(S["grid_chain"], 1)
            Q.sem_inc(S["out_stored"], 16)
            for s in stored:
                Q.sem_inc(s, 16)
            pool.wait_ge(S["const_in"], 16 * 6)
            pool.wait_ge(S["weights_split"], 4)
            blk(0, True, False, True)
            pool.wait_ge(S["grid_chain"], ITERS * GRID_CHAIN + 1)
            Q.tensor_copy(g_a[:, 0:1], g_a[:, 1:2]).then_inc(S["grid_done"], 1)
            with pool.Fori(1, NB - 1) as g:
                blk(g, True, True, True)
            blk(NB - 1, True, True, False)
            blk(NB, False, True, False)


def kernel(**inputs):
    import numpy as _np
    import concourse.bacc as _bacc
    from concourse import mybir as _mybir
    from concourse.bass_utils import run_bass_kernel_spmd as _run

    a = {k: _np.asarray(v) for k, v in inputs.items()}
    eye = _np.eye(P, dtype=_np.float32)

    def rows(w):
        return w.reshape(-1, P, w.shape[-1]).transpose(1, 0, 2)

    w1 = a["L1_ffn_w1"].reshape(E, D, 2, D).transpose(0, 3, 2, 1)
    w1 = w1.reshape(E, K, P, 2 * D).transpose(0, 2, 1, 3).reshape(E, P, 2 * K * D)
    w2 = a["L1_ffn_w2"].transpose(0, 2, 1).reshape(E, K, P, D).transpose(0, 2, 1, 3).reshape(E, P, K * D)
    moe = _np.concatenate([w1, w2], axis=2).reshape(E, P, 2, HALF).transpose(0, 2, 1, 3).reshape(2 * E, P, HALF)
    b1 = a["L1_ffn_b1"].reshape(E, K, P, 2).transpose(2, 0, 3, 1)
    arrays = {
        "x": a["x"].reshape(B, NB, TB, K, P).transpose(1, 4, 3, 0, 2).reshape(NB, P, K, N),
        "h0": a["cond_2048"].reshape(B, K, P).transpose(2, 1, 0),
        "grid": a["cond_2048"],
        "w_ih": rows(a["L0_cond_W_ih"]).reshape(P, -1),
        "w_hh": rows(a["L0_cond_W_hh"]).reshape(P, -1),
        "b_ih": a["L0_cond_b_ih"].reshape(G3, P).T,
        "b_hh": a["L0_cond_b_hh"].reshape(G3, P).T,
        "w_base": rows(a["L0_ffn_weight"].T).reshape(P, -1),
        "lora_a": rows(a["L0_ffn_lora_A"].reshape(E * RANK, D).T).reshape(P, -1),
        "lora_b": a["L0_ffn_lora_B"].transpose(0, 2, 1).reshape(E * RANK, D),
        "w_router": rows(a["L0_ffn_router_w"].T),
        "w_gate": rows(a["L1_ffn_gate_w"].T),
        "b_gate": a["L1_ffn_gate_b"].reshape(1, E),
        "w_moe": moe,
        "b1": b1,
        "b2": a["L1_ffn_b2"],
        "ident": eye,
        "sel_all": _np.repeat(eye[:E, :E], P, axis=1).reshape(E, E, P),
        "iota_e": _np.broadcast_to(_np.arange(E, dtype=_np.float32), (P, E)),
        "iota_f": (_np.arange(2 * D, dtype=_np.float32) % D - _np.repeat([0, 1], D)).astype(_np.float32).reshape(2 * K, P).T,
    }
    arrays = {k: _np.ascontiguousarray(v) for k, v in arrays.items()}
    nc = _bacc.Bacc("TRN2", target_bir_lowering=False, num_devices=1, dynamic_dma_scratch_size=2048)
    args = [nc.dram_tensor(f"in_{k}", v.shape, _mybir.dt.from_np(v.dtype), kind="ExternalInput").ap()
            for k, v in arrays.items()]
    out = nc.dram_tensor("out", (NB, P, K, N), F32, kind="ExternalOutput").ap()
    adaln_ffn_kernel(nc, *args, out)
    r = _run(nc, [{f"in_{k}": v for k, v in arrays.items()}], core_ids=[0])
    got = _np.asarray(r.results[0]["out"])
    return _np.ascontiguousarray(got.reshape(NB, P, K, B, TB).transpose(3, 0, 4, 2, 1).reshape(B, T, D))
```

```python
import numpy as np
import concourse.bass as bass
from concourse import mybir
from contextlib import ExitStack

F32 = mybir.dt.float32
F16 = mybir.dt.float16
I32 = mybir.dt.int32
U32 = mybir.dt.uint32
ACT = mybir.ActivationFunctionType
ALU = mybir.AluOpType

B, T, D = 4, 512, 512
P = 128
K = D // P
TB = 64
NB = T // TB
N = B * TB
G3 = 3 * K
E = 8
RANK = 16
HALF = (K * 2 * D + K * D) // 2
HEAD = 12
ITERS = 4
STEPS = (TB - HEAD) // ITERS
CHUNK = 768
CONV = 2 * 2 * HALF // CHUNK
GIB = G3 * N
SPAN = 8
LAP = 2 * SPAN
LAPS = TB // LAP
assert LAPS * 4 == 2 * E and LAPS == B and 2 * LAPS == NB
TT = N // P
LORA_SCALE = 32.0 / RANK

AS, WS = 16.0, 64.0
PS = AS * WS
YS = AS / (PS * PS)

LEAD = 8
FREE = LEAD - 1

ORDER = [("up", 0), ("up", 1), ("down", 0), ("up", 2), ("down", 1), ("up", 3), ("down", 2),
         ("up", 4), ("down", 3), ("up", 5), ("down", 4), ("up", 6), ("down", 5), ("up", 7),
         ("down", 6), ("down", 7)]
EARLY = 3
BASE_CUT = (0, 0, 24, 38, 48)
PARTS = ((0, 0), (1, 0), (0, 1))
UP = [(half, k, w, a) for half in range(2) for k in range(K) for w, a in PARTS]
DOWN = [(h, w, a) for h in range(K) for w, a in PARTS]
LOW = [(t, k, w, a) for t in range(TT) for k in range(K) for w, a in PARTS]
GI = [(k, w, a) for k in range(K) for w, a in PARTS]
BASE = [(o, k, w, a) for o in range(K) for k in range(K) for w, a in PARTS]
SIZE = {"up": len(UP), "down": len(DOWN), "gi": len(GI)}


def pieces(order, slots):
    flat = [(kind, i, j) for kind, i in order for j in range(SIZE[kind])]
    return [flat[s * len(flat) // slots:(s + 1) * len(flat) // slots] for s in range(slots)]


def ended(slots, kind):
    return [[i for k, i, j in slot if k == kind and j == SIZE[kind] - 1] for slot in slots]


def adaln_ffn_kernel(nc, x, h0, grid, w_ih, w_hh, b_ih, b_hh, w_base, lora_a, lora_b, w_router,
                     w_gate, b_gate, w_moe, b1, b2, ident, sel_all, iota_e, iota_f, out):
    scratch = nc.dram_tensor("moe_split", (2 * E, P, 2, HALF), F16).ap()
    gates_in = nc.dram_tensor("gates_in", (NB, P, GIB), F32).ap()
    ctx = ExitStack()
    with ctx:
        def sb(name, shape, dt):
            return ctx.enter_context(nc.sbuf_tensor(name, shape, dt))

        def pb(name):
            return ctx.enter_context(nc.psum_tensor(name, [P, 512], F32))

        def sem(name):
            return ctx.enter_context(nc.semaphore(name))

        whh = sb("whh", [P, 2, K, 3 * D], F16)
        wih = sb("wih", [P, 2, K, 3 * D], F16)
        wm = sb("wm", [P, 2, 2, 2, HALF], F16)
        wbase = sb("wbase", [P, 2, K, D], F16)
        wla = sb("wla", [P, 2, K, P], F16)
        wlb = sb("wlb", [P, 2, D], F16)
        gm = sb("gm", [P, 2, B, K, D], F16)
        wr = sb("wr", [P, K, E], F32)
        wg = sb("wg", [P, K, E], F32)
        bg16 = sb("bg16", [P, E], F32)
        idt = sb("idt", [P, P], F32)
        sela = sb("sela", [E, E, P], F16)
        iote = sb("iote", [P, E], F32)
        iotf = sb("iotf", [P, 2 * K], F32)
        bi = sb("bi", [P, G3], F32)
        bh = sb("bh", [P, G3], F32)
        bn = sb("bn", [P, K, B], F32)
        b1s = sb("b1s", [P, E, 2, K], F32)
        b1sig = sb("b1sig", [P, E, K], F32)
        b2s = sb("b2s", [E, 2, D], F16)
        gi = sb("gi", [P, 2 * GIB + TB], F32)
        xr = sb("xr", [P, K, N], F32)
        hf = sb("hf", [P, K, B, TB], F32)
        hx = sb("hx", [P, K, N], F32)
        hxs = sb("hxs", [P, 2, K, N], F16)
        x1 = sb("x1", [P, K, N], F32)
        x1s = sb("x1s", [P, 2, K, N], F16)
        xs = (hxs, x1s)
        wb = sb("wb", [P, 2, N], F32)
        stage_l0 = sb("stage_l0", [P, K * D], F32)
        stage_grid = sb("stage_grid", [P, 3 * D], F32)
        axw = sb("axw", [P, TT, E, RANK], F32)
        axs = sb("axs", [P, 2, N], F16)
        glu = sb("glu", [P, 2, N], F32)
        lin = sb("lin", [P, 2, N], F32)
        ys = sb("ys", [P, 2, 2, N], F16)
        h = sb("h", [P, K, B], F32)
        hs = sb("hs", [P, K, 2, B], F16)
        part = sb("part", [P, 3, K, B], F32)
        now = sb("now", [P, G3, B], F32)
        pre = sb("pre", [P, 3, K, B], F32)
        rg = sb("rg", [P, K, B], F32)
        zg = sb("zg", [P, K, B], F32)
        ng = sb("ng", [P, K, B], F32)
        rn = sb("rn", [P, K, B], F32)
        na = sb("na", [P, K, B], F32)
        dh = sb("dh", [P, K, B], F32)
        zd = sb("zd", [P, K, B], F32)
        lg = sb("lg", [P, TT, E], F32)
        top = sb("top", [P, TT, E], F32)
        tix = sb("tix", [P, TT, E], U32)
        tif = sb("tif", [P, TT, 2], F32)
        tdf = sb("tdf", [P, TT, 2], F32)
        tpr = sb("tpr", [P, TT, 2], F32)
        tw = sb("tw", [P, 3, TT, E], F32)
        wt = sb("wt", [E, 2, N], F16)
        hf_cols = hf[:, :, :, :].rearrange("p k b t -> p k (b t)")
        sela32 = hf[0:E].rearrange("p k b t -> p (k b t)").rearrange("p (e n) -> p e n", n=P)
        b2f = hx[0:E, 0:2, :].rearrange("p k n -> p (k n)")
        wm32 = [wm[:, i].rearrange("p a b n -> p (a b n)").bitcast(F32) for i in range(2)]
        st_la = glu[:, :, :].rearrange("p k n -> p (k n)")
        st_lb = lin[:, :, :].rearrange("p k n -> p (k n)")
        flat = stage_grid[:, :].rearrange("p (a n) -> p a n", n=D)
        g_w1, g_i1, g_t = (flat[:, i] for i in range(3))
        g_in = ys[:, :, :, :].rearrange("p a l n -> p (a l n)").bitcast(F32)
        flat2 = x1[:, :, :].rearrange("p k n -> p (k n)").rearrange("p (a n) -> p a n", n=D)
        g_i0, g_w0 = flat2[:, 0], flat2[:, 1]
        g_int = hx[:, 0:2, :].rearrange("p k n -> p (k n)").bitcast(I32)
        g_a = hx[:, 2:4, :].rearrange("p k n -> p (k n)")

        bank_g = [pb(f"bank_g{i}") for i in range(3)]
        bank_wb = pb("bank_wb")
        bank_acc = [pb(f"bank_acc{i}") for i in range(2)]
        bank_up = [pb(f"bank_up{i}") for i in range(2)]
        pg = [b[:, 0:K * 2 * B].rearrange("p (j s b) -> p j s b", s=2, b=B) for b in bank_g]
        p_log = bank_wb[:, 0:TT * E].rearrange("p (t e) -> p t e", e=E)
        p_wt = bank_acc[0][0:E, 0:N]
        p_ax = bank_acc[0][:, 0:N].rearrange("p (t e r) -> p t e r", e=E, r=RANK)
        p_wb = bank_wb[:, :].rearrange("p (e n) -> p e n", n=N)
        gi_bank = (bank_wb, bank_acc[0], bank_acc[1], bank_up[0])

        names = """
            const_in bias_in l0_in x_in grid_in gi_in
            setup_dve wih_hi whh_hi b2_hi l0_hi wih_split whh_split b2_split sel_ready l0_split moe_lo moe_hi
            h_ready gates_mm r_pre n_pre z_pre r_done n_done z_done gru_chain h_kept
            x_hi x_split gi_mm gi_done
            hx_copied h_hi h_lo router_mm top_diff top_prob dense_w top_chain
            ax_mm axw_done axt_mm ax_hi ax_lo l0_mm x1_done x1_hi x1_lo
            sample_mm sample_done sample_hi sample_lo wt_mm wt_hi wt_lo wb_mm wb_done
            up_mm sig_done act_done y_done y_hi y_lo down_mm final_done out_stored
            grid_chain
        """.split()
        S = {n: sem(n) for n in names}
        stage_in = [sem("stage_in_a"), sem("stage_in_b")]
        stored = [sem("stored_a"), sem("stored_b")]
        gi_stored = [sem("gi_stored_a"), sem("gi_stored_b")]
        w_in = [sem("w_in_a"), sem("w_in_b")]
        wih_in = [sem(f"wih_in_{gate}") for gate in "rzn"]
        whh_in = [sem(f"whh_in_{gate}") for gate in "rzn"]

        passed = {e.engine: sem(f"passed_{n}") for n, e in (("dve", nc.vector), ("pool", nc.gpsimd))}

        block = ctx.enter_context(nc.Block())
        TOP_CHAIN = 2 + 4 * TT
        GRU_CHAIN = 9
        GRID_CHAIN = 11 + 7 * K
        PAIR = pieces(ORDER, STEPS)
        UPS = ended(PAIR, "up")
        GIS = pieces([("gi", m) for m in range(G3)], SPAN)
        GI_ENDS = ended(GIS, "gi")

        def part_of(w, q):
            return w.rearrange("p (k n) -> p k n", k=K)[:, :, q * D:(q + 1) * D]

        def apart(engine):
            engine.sem_inc(passed[engine.engine], 1)

        @block.sync
        def _(sp):
            for q in range(3):
                sp.dma_start(part_of(wm32[0], q), part_of(w_ih, q)).then_inc(wih_in[q], 16)
                if q == 0:
                    sp.dma_start(xr[:, :, :], x[0]).then_inc(S["x_in"], 16)
                    for dst, src in ((bi[:, :], b_ih), (bh[:, :], b_hh), (h[:, :, :], h0),
                                     (b1s[:, :, :, :], b1), (b2f, b2),
                                     (bg16[:, :], b_gate.to_broadcast([P, E]))):
                        sp.dma_start(dst, src).then_inc(S["bias_in"], 16)
            for q in range(3):
                sp.dma_start(part_of(wm32[1], q), part_of(w_hh, q)).then_inc(whh_in[q], 16)
            for dst, src in ((idt[:, :], ident), (sela32[:, :, :], sel_all),
                             (iote[:, :], iota_e), (iotf[:, :], iota_f), (wr[:, :, :], w_router),
                             (wg[:, :, :], w_gate)):
                sp.dma_start(dst, src).then_inc(S["const_in"], 16)

            def at(i):
                return bass.ds(i, 1) if not isinstance(i, int) else slice(i, i + 1)

            def load_x(v):
                sp.wait_ge(S["x_split"], v)
                sp.dma_start(xr[:, :, :], x[at(v * (NB - 1) % NB)]).then_inc(S["x_in"], 16)

            def load_half(n, par):
                sp.dma_start(wm32[0][:, par * HALF:(par + 1) * HALF], w_moe[at(n)]).then_inc(stage_in[par], 16)

            load_x(1)
            sp.wait_ge(S["wih_split"], 3)
            load_half(0, 0)
            sp.wait_ge(S["whh_split"], 3)
            load_half(1, 1)
            load_x(2)
            sp.dma_start(g_in, grid[0:1].to_broadcast([P, D])).then_inc(S["grid_in"], 16)
            for dst, src in ((stage_l0[:, :], w_base), (st_la, lora_a), (st_lb, lora_b)):
                sp.dma_start(dst, src).then_inc(S["l0_in"], 16)

            def lap(it, more):
                for q in range(4):
                    v = it * 2 + (1 + q // 2)
                    if more and q % 2 == 0:
                        load_x(v + 2)
                    if more and q == 1:
                        sp.wait_ge(S["grid_chain"], it * GRID_CHAIN + 2)
                        sp.dma_start(g_in, grid[at(it + 1)].to_broadcast([P, D])).then_inc(S["grid_in"], 16)
                    n = it * 4 + q
                    sp.wait_ge(S["moe_lo"], (it * 4 + (q + 1)) * (HALF // CHUNK))
                    sp.dma_start(scratch[at(n)], wm[:, 1, q % 2]).then_inc(stored[q % 2], 16)
                    if more or q < 2:
                        load_half(it * 4 + (q + 2), q % 2)
                    if more:
                        sp.wait_ge(S["gi_done"], v * G3 + (q % 2 + 1) * (G3 // 2))
                        sl = slice((q % 2) * GIB // 2, (q % 2 + 1) * GIB // 2)
                        sp.dma_start(gates_in[at(v * (NB - 1) % NB), :, sl],
                                     gi[:, GIB + sl.start:GIB + sl.stop]).then_inc(gi_stored[q % 2], 16)

            with sp.Fori(0, LAPS - 1) as it:
                lap(it, True)
            lap(LAPS - 1, False)
            for par in range(2):
                sp.wait_ge(stored[par], 16 * E + 16)
                sp.wait_ge(gi_stored[par], 16 * (NB - 2) + 16)

            experts = scratch.rearrange("(e h) p l n -> e p h (l n)", h=2)

            def ffn_block(f, gi_next, x_next):
                if gi_next:
                    sp.wait_ge(S["h_ready"], f * TB + (TB + 1))
                    sp.dma_start(gi[:, bass.ds(f % 2 * GIB, GIB)],
                                 gates_in[at(f + 2)]).then_inc(S["gi_in"], 16)
                with sp.Fori(0, ITERS) as it:
                    for e in range(2):
                        sp.wait_ge(S["down_mm"], f * 32 + it * 8 + K * (e + 1))
                        sp.dma_start(wm[:, e].rearrange("p h l n -> p h (l n)"),
                                     experts[bass.ds(it * 2 + e, 1)]).then_inc(w_in[e], 16)
                if x_next:
                    sp.wait_ge(S["x1_done"], f * 2 + 2)
                    sp.dma_start(xr[:, :, :], x[at(f + 1)]).then_inc(S["x_in"], 16)
                sp.wait_ge(S["final_done"], f * 2 + 2)
                sp.dma_start(out[at(f)], x1[:, :, :]).then_inc(S["out_stored"], 16)

            with sp.Fori(0, NB - 2) as f:
                ffn_block(f, True, True)
            ffn_block(NB - 2, False, True)
            ffn_block(NB - 1, False, False)
            sp.wait_ge(S["out_stored"], 16 * NB + 16)

        @block.tensor
        def _(pe):
            mm = nc.tensor.matmul

            def gru(t, early=None):
                pe.wait_ge(S["h_ready"], t + 1)
                for g in (0, 2, 1):
                    if g == 1 and early:
                        early()
                    for j in range(K):
                        col = (g * K + j) * P
                        for k in range(K):
                            for w in range(2):
                                last = mm(pg[g][:, j], whh[:, w, k, col:col + P], hs[:, k],
                                          start=(k == 0 and w == 0), stop=(k == K - 1 and w == 1))
                    last.then_inc(S["gates_mm"], 1)

            def gi_piece(v, par, m, j):
                k, w, a = GI[j]
                if j == 0 and not (isinstance(v, int) and v * G3 + m < len(gi_bank)):
                    pe.wait_ge(S["gi_done"], v * G3 + (m + 1 - len(gi_bank)))
                i = mm(gi_bank[m % len(gi_bank)][:, 0:N], wih[:, w, k, m * P:(m + 1) * P],
                       xs[par][:, a, k],
                       start=(j == 0), stop=(j == len(GI) - 1))
                if j == len(GI) - 1:
                    i.then_inc(S["gi_mm"], 1)

            def up_piece(f, it, i, j):
                half, k, w, a = UP[j]
                e, tile = i // K, i % K
                if j == 0:
                    if tile == 0:
                        pe.wait_ge(w_in[e], (f * ITERS + it + 1) * 16)
                    if i == 0:
                        pe.wait_ge(S["sample_lo"], f + 2)
                    pe.wait_ge(S["act_done"], f * 32 + it * 8 + (i + FREE))
                at = k * 2 * D + half * D + tile * P
                r = mm(bank_up[i % 2][:, half * N:(half + 1) * N],
                       wm[:, e, at // HALF, w, at % HALF:at % HALF + P], hxs[:, a, k],
                       start=(k == 0 and w == 0 and a == 0), stop=(k == K - 1 and a == 1))
                if j == len(UP) - 1:
                    r.then_inc(S["up_mm"], 1)

            def down_piece(f, it, i, j):
                hh, w, a = DOWN[j]
                e, tile = i // K, i % K
                if j == 0:
                    pe.wait_ge(S["y_lo"], f * 32 + it * 8 + (i + 1 + LEAD))
                at = K * 2 * D + tile * D + hh * P
                r = mm(bank_acc[hh // 2][:, (hh % 2) * N:(hh % 2 + 1) * N],
                       wm[:, e, at // HALF, w, at % HALF:at % HALF + P], ys[:, i % 2, a],
                       start=False, stop=False, skip_group_check=True)
                if j == len(DOWN) - 1:
                    r.then_inc(S["down_mm"], 1)

            def base(f, first, last_):
                for o, k, w, a in BASE[first:last_]:
                    mm(bank_up[o // 2][:, (o % 2) * N:(o % 2 + 1) * N], wbase[:, w, k, o * P:(o + 1) * P], hxs[:, a, k],
                       start=(o % 2 == 0 and k == 0 and w == 0 and a == 0), stop=False, skip_group_check=True)

            def sample(first, last_):
                for l in range(first, last_):
                    for b in range(B):
                        dst = bank_acc[l // 2][:, (l % 2) * N + b * TB:(l % 2) * N + (b + 1) * TB]
                        for k in range(K):
                            for w, a in PARTS:
                                i = mm(dst, gm[:, w, b, k, l * P:(l + 1) * P], x1s[:, a, k, b * TB:(b + 1) * TB],
                                       start=(k == 0 and w == 0 and a == 0), stop=(k == K - 1 and a == 1))
                i.then_inc(S["sample_mm"], 1)

            def logits(w):
                for tt in range(TT):
                    for k in range(K):
                        i = mm(p_log[:, tt], hx[:, k, tt * P:(tt + 1) * P], w[:, k], start=(k == 0), stop=(k == K - 1))
                i.then_inc(S["router_mm"], 1)

            def head(s, f):
                if s == 0:
                    pe.wait_ge(S["h_hi"], f + 1)
                    pe.wait_ge(S["hx_copied"], f + 1)
                    logits(wr)
                if s == 1:
                    pe.wait_ge(S["h_lo"], f + 1)
                    for tt, k, w, a in LOW:
                        i = mm(bank_acc[0][:, tt * P:(tt + 1) * P], hxs[:, a, k, tt * P:(tt + 1) * P], wla[:, w, k],
                               start=(k == 0 and w == 0 and a == 0), stop=(k == K - 1 and a == 1))
                    i.then_inc(S["ax_mm"], 1)
                if s in (1, 2, 3, 4):
                    base(f, BASE_CUT[s - 1], BASE_CUT[s])
                if s == 3:
                    pe.wait_ge(S["axw_done"], f + 1)
                    for tt in range(TT):
                        i = mm(bank_acc[1][:, tt * P:(tt + 1) * P], axw[:, tt].rearrange("p e r -> p (e r)"), idt[:, :],
                               start=True, stop=True)
                    i.then_inc(S["axt_mm"], 1)
                if s == 4:
                    pe.wait_ge(S["ax_lo"], f + 1)
                    for o in range(K):
                        for w, a in PARTS:
                            i = mm(bank_up[o // 2][:, (o % 2) * N:(o % 2 + 1) * N], wlb[:, w, o * P:(o + 1) * P], axs[:, a],
                                   start=False, stop=(a == 1), skip_group_check=True)
                    i.then_inc(S["l0_mm"], 1)
                if s == 6:
                    pe.wait_ge(S["x1_lo"], f + 1)
                    sample(0, 2)
                if s == 7:
                    sample(2, 4)
                if s == 8:
                    pe.wait_ge(S["sample_done"], f * 2 + 2)
                    logits(wg)
                if s == 10:
                    pe.wait_ge(S["dense_w"], f * 2 + 2)
                    for tt in range(TT):
                        i = mm(p_wt[:, tt * P:(tt + 1) * P], tw[:, 2, tt], idt[:, :], start=True, stop=True)
                    i.then_inc(S["wt_mm"], 1)
                if s == 11:
                    pe.wait_ge(S["wt_lo"], f + 1)
                    for hh in range(K):
                        for w, a in PARTS:
                            mm(bank_acc[hh // 2][:, (hh % 2) * N:(hh % 2 + 1) * N], b2s[:, w, hh * P:(hh + 1) * P], wt[:, a],
                               start=(hh % 2 == 0 and w == 0 and a == 0), stop=False, skip_group_check=True)

            def weights_over_partitions(f, it):
                pe.wait_ge(S["wb_done"], f * ITERS + it + 1)
                for e in range(2):
                    n = it * 2 + e
                    pick = sela[:, n] if isinstance(n, int) else sela[:, bass.ds(n, 1)]
                    for a in range(2):
                        i = mm(p_wb[:, e], pick, wt[:, a], start=(a == 0), stop=(a == 1))
                i.then_inc(S["wb_mm"], 1)

            def lap(it, visits):
                for s in range(LAP):
                    c = s // SPAN
                    gru(it * LAP + s)
                    if c < visits:
                        if s % SPAN == 0:
                            pe.wait_ge(S["x_split"], it * 2 + (2 + c))
                        for _, m, j in GIS[s % SPAN]:
                            gi_piece(it * 2 + (1 + c), (1 + c) % 2, m, j)

            def blk(g):
                f = g - 1
                for s in range(HEAD):
                    gru(g * TB + s)
                    head(s, f)
                with pe.Fori(0, ITERS) as it:
                    def pieces_of(some):
                        for kind, i, j in some:
                            (up_piece if kind == "up" else down_piece)(f, it, i, j)

                    for s in range(STEPS):
                        gru(g * TB + it * STEPS + (HEAD + s), lambda: pieces_of(PAIR[s][:EARLY]))
                        if s == 0:
                            weights_over_partitions(f, it)
                        pieces_of(PAIR[s][EARLY:])

            def last_blk(f):
                def up(it, i):
                    for j in range(SIZE["up"]):
                        up_piece(f, it, i, j)

                def down(it, i):
                    for j in range(SIZE["down"]):
                        down_piece(f, it, i, j)

                def pair(it, more):
                    for i in range(2, 2 * K):
                        down(it, i - 2)
                        up(it, i)
                    down(it, 2 * K - 2)
                    if more:
                        weights_over_partitions(f, it + 1)
                        up(it + 1, 0)
                    down(it, 2 * K - 1)
                    if more:
                        up(it + 1, 1)

                for s in range(HEAD):
                    head(s, f)
                    if s >= HEAD - 2:
                        up(0, s - (HEAD - 2))
                weights_over_partitions(f, 0)
                with pe.Fori(0, ITERS - 1) as it:
                    pair(it, True)
                pair(ITERS - 1, False)

            pe.wait_ge(S["x_split"], 1)
            for m in range(G3):
                if m % K == 0:
                    pe.wait_ge(S["wih_split"], m // K + 1)
                for j in range(len(GI)):
                    gi_piece(0, 0, m, j)
            pe.wait_ge(S["whh_split"], 3)
            with pe.Fori(0, LAPS - 1) as it:
                lap(it, 2)
            lap(LAPS - 1, 1)
            pe.wait_ge(S["const_in"], 16 * 6)
            pe.wait_ge(S["l0_split"], 3)
            pe.wait_ge(S["grid_chain"], LAPS * GRID_CHAIN + 1)
            with pe.Fori(1, NB) as g:
                blk(g)
            last_blk(NB - 1)

        @block.scalar
        def _(act):
            def run(dst, src, func, **kw):
                return nc.scalar.activation(dst, src, func, **kw)

            def gru_r(t):
                act.wait_ge(S["r_pre"], t + 1)
                run(rg[:, :, :], pre[:, 0], ACT.Sigmoid, scale=1 / PS).then_inc(S["r_done"], 1)

            def gru_nz(t):
                act.wait_ge(S["n_pre"], t + 1)
                run(ng[:, :, :], na[:, :, :], ACT.Tanh, scale=1 / PS).then_inc(S["n_done"], 1)
                act.wait_ge(S["z_pre"], t + 1)
                run(zg[:, :, :], pre[:, 1], ACT.Sigmoid, scale=1 / PS).then_inc(S["z_done"], 1)

            def gi_out(v, m, half):
                act.wait_ge(S["gi_mm"], v * G3 + (m + 1))
                if half and m % (G3 // 2) == 0:
                    act.wait_ge(gi_stored[m // (G3 // 2)], v * 16)
                run(gi[:, half * GIB + m * N:half * GIB + (m + 1) * N], gi_bank[m % len(gi_bank)][:, 0:N],
                    ACT.Identity, bias=bi[:, m:m + 1]).then_inc(S["gi_done"], 1)

            def x_hi(v, par):
                act.wait_ge(S["x_in"], v * 16 + 16)
                if not (isinstance(v, int) and v < 2):
                    act.wait_ge(S["gi_mm"], v * G3 - G3)
                run(xs[par][:, 0], xr[:, :, :], ACT.Copy, scale=AS).then_inc(S["x_hi"], 1)

            def head_start(f):
                act.wait_ge(S["h_kept"], f * TB + (TB + 1))
                act.wait_ge(S["sample_lo"], f + 1)
                run(hx[:, 0:K // 2, :], hf_cols[:, 0:K // 2], ACT.Copy)
                act.wait_ge(S["down_mm"], f * 32 + LEAD)
                run(hxs[:, 0], hf_cols, ACT.Copy).then_inc(S["h_hi"], 1)

            def head_mid(s, f):
                if s == 5:
                    act.wait_ge(S["x1_done"], f * 2 + 2)
                    run(x1s[:, 0], x1[:, :, :], ACT.Copy, scale=AS).then_inc(S["x1_hi"], 1)
                if s == 9:
                    run(hxs[:, 0], hx[:, :, :], ACT.Copy).then_inc(S["sample_hi"], 1)

            def head_end(s, f):
                if s in (1, 8):
                    which = int(s == 8)
                    act.wait_ge(S["top_diff"], f * 2 + which + 1)
                    run(tpr[:, :, :], tdf[:, :, :], ACT.Sigmoid, scale=1 / AS).then_inc(S["top_prob"], 1)
                if s == 3:
                    act.wait_ge(S["axt_mm"], f + 1)
                    run(axs[:, 0], bank_acc[1][:, 0:N], ACT.Copy, scale=LORA_SCALE / WS).then_inc(S["ax_hi"], 1)
                if s in (6, 7):
                    q = s - 6
                    act.wait_ge(S["sample_mm"], f * 2 + (q + 1))
                    run(hx[:, 2 * q:2 * q + 2, :].rearrange("p k n -> p (k n)"), bank_acc[q][:, :], ACT.Copy,
                        scale=1 / WS).then_inc(S["sample_done"], 1)
                if s == 10:
                    act.wait_ge(S["wt_mm"], f + 1)
                    run(wt[:, 0], p_wt, ACT.Copy, scale=AS).then_inc(S["wt_hi"], 1)

            def tile_mid(f, it, i):
                act.wait_ge(S["y_done"], f * 32 + it * 8 + (i + 1 + LEAD))
                act.wait_ge(S["down_mm"], f * 32 + it * 8 + (i + FREE))
                run(ys[:, i % 2, 0], lin[:, i % 2], ACT.Copy).then_inc(S["y_hi"], 1)

            def tile_end(f, it, i):
                act.wait_ge(S["up_mm"], f * 32 + it * 8 + (i + 1))
                act.wait_ge(S["y_done"], f * 32 + it * 8 + (i + FREE))
                run(glu[:, i % 2], bank_up[i % 2][:, 0:N], ACT.Sigmoid, scale=1.702 / PS,
                    bias=b1sig[:, bass.ds(it * 2 + i // K, 1), i % K]).then_inc(S["sig_done"], 1)

            def l0_hi(q):
                act.wait_ge(S["l0_in"], 48)
                dst, src = ((wbase[:, 0].rearrange("p k n -> p (k n)"), stage_l0[:, :]),
                            (wla[:, 0].rearrange("p k n -> p (k n)"), st_la), (wlb[:, 0], st_lb))[q]
                run(dst, src, ACT.Copy, scale=WS).then_inc(S["l0_hi"], 1)

            def lap(it, visits):
                for s in range(LAP):
                    gru_r(it * LAP + s)
                    gru_nz(it * LAP + s)
                    for c in range(CONV):
                        if c * LAP // CONV == s:
                            moe_hi(it, c)
                    c, at = s // SPAN, s % SPAN
                    if c < visits:
                        for m in (GI_ENDS[at - 1] if at else []) + (GI_ENDS[at] if at == SPAN - 1 else []):
                            gi_out(it * 2 + (1 + c), m, 1)
                    if visits == 2 and at == 1:
                        x_hi(it * 2 + (2 + c), c % 2)
                    if visits == 1 and s in (9, 10, 11):
                        l0_hi(s - 9)

            def blk(g, gru_on):
                f = g - 1
                head_start(f)
                for s in range(HEAD):
                    if gru_on:
                        gru_r(g * TB + s)
                    head_mid(s, f)
                    if gru_on:
                        gru_nz(g * TB + s)
                    head_end(s, f)
                with act.Fori(0, ITERS) as it:
                    for s in range(STEPS):
                        t = g * TB + it * STEPS + (HEAD + s)
                        if gru_on:
                            gru_r(t)
                        if s:
                            for i in UPS[s - 1]:
                                tile_mid(f, it, i)
                        if gru_on:
                            gru_nz(t)
                        for i in UPS[s]:
                            tile_end(f, it, i)
                    assert not UPS[STEPS - 1]

            def moe_hi(it, c):
                per = HALF // CHUNK
                q = c // per
                if c % per == 0:
                    act.wait_ge(stage_in[q % 2], (it * 2 + (q // 2 + 1)) * 16)
                    act.wait_ge(stored[q % 2], (it * 2 + (q // 2 + 1)) * 16)
                at = (c % per) * CHUNK
                run(wm[:, 1, q % 2, 0, at:at + CHUNK], wm32[0][:, (q % 2) * HALF + at:(q % 2) * HALF + at + CHUNK],
                    ACT.Copy, scale=WS).then_inc(S["moe_hi"], 1)

            for q in range(3):
                act.wait_ge(wih_in[q], 16)
                run(part_of(wih[:, 0].rearrange("p k n -> p (k n)"), q), part_of(wm32[0], q), ACT.Copy,
                    scale=WS).then_inc(S["wih_hi"], 1)
                if q == 0:
                    x_hi(0, 0)
            act.wait_ge(S["setup_dve"], 2)
            for q in range(3):
                act.wait_ge(whh_in[q], 16)
                run(part_of(whh[:, 0].rearrange("p k n -> p (k n)"), q), part_of(wm32[1], q), ACT.Copy,
                    scale=WS).then_inc(S["whh_hi"], 1)
                for m in range(q * K, (q + 1) * K):
                    gi_out(0, m, 0)
                if q == 0:
                    act.wait_ge(S["bias_in"], 16 * 6)
                    run(b2s[:, 0], b2f, ACT.Copy, scale=WS).then_inc(S["b2_hi"], 1)
            x_hi(1, 1)
            act.wait_ge(S["const_in"], 16 * 6)
            run(sela[:, :, :], sela32[:, :, :], ACT.Copy).then_inc(S["sel_ready"], 1)
            with act.Fori(0, LAPS - 1) as it:
                lap(it, 2)
            lap(LAPS - 1, 1)
            act.wait_ge(S["grid_chain"], LAPS * GRID_CHAIN + 1)
            with act.Fori(1, NB) as g:
                blk(g, True)
            blk(NB, False)

        @block.vector
        def _(dve):
            V = nc.vector
            tt_, ts_, stt_ = V.tensor_tensor, V.tensor_scalar, V.scalar_tensor_tensor

            def gru(t, base):
                n = [0]

                def link(i, *also):
                    n[0] += 1
                    i.then_inc(S["gru_chain"], 1)
                    for name in also:
                        dve.wait_ge(S[name], t + 1)
                    dve.wait_ge(S["gru_chain"], t * GRU_CHAIN + n[0])

                window = gi[:, bass.ds(base, GIB)].rearrange("p (m b t) -> p m b t", b=B, t=TB)

                def gates(g):
                    return now[:, g * K:(g + 1) * K]

                link(V.tensor_copy(now[:, :, :], window[:, :, :, 0:1]))

                dve.wait_ge(S["gates_mm"], t * 3 + 1)
                link(tt_(part[:, 0], pg[0][:, :, 0], gates(0), ALU.add))
                tt_(pre[:, 0], pg[0][:, :, 1], part[:, 0], ALU.add).then_inc(S["r_pre"], 1)
                dve.wait_ge(S["h_kept"], t + 1)
                dve.wait_ge(S["gates_mm"], t * 3 + 2)
                link(tt_(part[:, 2], pg[2][:, :, 0], bn[:, :, :], ALU.add))
                link(tt_(pre[:, 2], pg[2][:, :, 1], part[:, 2], ALU.add), "r_done")
                link(tt_(rn[:, :, :], pre[:, 2], rg[:, :, :], ALU.mult))
                tt_(na[:, :, :], rn[:, :, :], gates(2), ALU.add).then_inc(S["n_pre"], 1)
                dve.wait_ge(S["gates_mm"], t * 3 + 3)
                link(tt_(part[:, 1], pg[1][:, :, 0], gates(1), ALU.add))
                tt_(pre[:, 1], pg[1][:, :, 1], part[:, 1], ALU.add).then_inc(S["z_pre"], 1)
                dve.wait_ge(S["n_done"], t + 1)
                link(stt_(dh[:, :, :], ng[:, :, :], -AS, h[:, :, :], ALU.mult, ALU.add), "z_done")
                link(tt_(zd[:, :, :], dh[:, :, :], zg[:, :, :], ALU.mult))
                stt_(hs[:, :, 0], ng[:, :, :], AS, zd[:, :, :], ALU.mult, ALU.add)
                link(stt_(h[:, :, :], ng[:, :, :], AS, zd[:, :, :], ALU.mult, ALU.add))
                tt_(hs[:, :, 1], h[:, :, :], hs[:, :, 0], ALU.subtract).then_inc(S["h_ready"], 1)
                assert n[0] == GRU_CHAIN, n

            def x_lo(v, par):
                dve.wait_ge(S["x_hi"], v + 1)
                stt_(xs[par][:, 1], xr[:, :, :], AS, xs[par][:, 0], ALU.mult, ALU.subtract).then_inc(S["x_split"], 1)

            def top_a(which, f):
                base = (f * 2 + which) * TOP_CHAIN
                dve.wait_ge(S["router_mm"], f * 2 + which + 1)
                if which:
                    tt_(lg[:, :, :], p_log, bg16[:, :].unsqueeze(1).to_broadcast([P, TT, E]), ALU.add
                        ).then_inc(S["top_chain"], 1)
                else:
                    V.tensor_copy(lg[:, :, :], p_log).then_inc(S["top_chain"], 1)
                dve.wait_ge(S["top_chain"], base + 1)
                apart(dve)
                for tt in range(TT):
                    V.max(top[:, tt], lg[:, tt]).then_inc(S["top_chain"], 1)
                dve.wait_ge(S["top_chain"], base + (1 + TT))
                apart(dve)
                for tt in range(TT):
                    V.max_index(tix[:, tt], top[:, tt], lg[:, tt]).then_inc(S["top_chain"], 1)
                tt_(tdf[:, :, 0:1], top[:, :, 0:1], top[:, :, 1:2], ALU.subtract)
                tt_(tdf[:, :, 1:2], top[:, :, 1:2], top[:, :, 0:1], ALU.subtract).then_inc(S["top_diff"], 1)
                dve.wait_ge(S["top_chain"], base + (1 + 2 * TT))
                V.tensor_copy(tif[:, :, :], tix[:, :, 0:2]).then_inc(S["top_chain"], 1)

            def top_b(which, f):
                base = (f * 2 + which) * TOP_CHAIN
                dve.wait_ge(S["top_chain"], base + (2 + 2 * TT))
                dve.wait_ge(S["top_prob"], f * 2 + which + 1)
                for tt in range(TT):
                    for c in range(2):
                        ts_(tw[:, c, tt], iote[:, :], tif[:, tt, c:c + 1], tpr[:, tt, c:c + 1], ALU.is_equal, ALU.mult
                            ).then_inc(S["top_chain"], 1)
                dve.wait_ge(S["top_chain"], base + TOP_CHAIN)
                tt_(tw[:, 2], tw[:, 0], tw[:, 1], ALU.add).then_inc(S["dense_w"], 1)
                if not which:
                    dve.wait_ge(S["dense_w"], f * 2 + 1)
                    dve.wait_ge(S["ax_mm"], f + 1)
                    tt_(axw[:, :, :, :], p_ax, tw[:, 2].unsqueeze(3).to_broadcast([P, TT, E, RANK]),
                        ALU.mult).then_inc(S["axw_done"], 1)

            def head(s, f):
                if s == 0:
                    dve.wait_ge(S["h_hi"], f + 1)
                    tt_(hxs[:, 1], hf_cols, hxs[:, 0], ALU.subtract).then_inc(S["h_lo"], 1)
                if s in (1, 8):
                    top_a(int(s == 8), f)
                if s in (2, 9):
                    top_b(int(s == 9), f)
                if s == 3:
                    dve.wait_ge(S["ax_hi"], f + 1)
                    stt_(axs[:, 1], bank_acc[1][:, 0:N], LORA_SCALE / WS, axs[:, 0], ALU.mult,
                         ALU.subtract).then_inc(S["ax_lo"], 1)
                if s == 4:
                    dve.wait_ge(S["l0_mm"], f + 1)
                    dve.wait_ge(S["x_in"], f * 16 + (NB + 1) * 16)
                    dve.wait_ge(S["out_stored"], f * 16 + 16)
                    for q in range(2):
                        sl = slice(2 * q, 2 * q + 2)
                        stt_(x1[:, sl, :].rearrange("p k n -> p (k n)"), bank_up[q][:, :], 1 / PS,
                             xr[:, sl, :].rearrange("p k n -> p (k n)"), ALU.mult, ALU.add).then_inc(S["x1_done"], 1)
                if s == 5:
                    dve.wait_ge(S["x1_hi"], f + 1)
                    stt_(x1s[:, 1], x1[:, :, :], AS, x1s[:, 0], ALU.mult, ALU.subtract).then_inc(S["x1_lo"], 1)
                if s == 10:
                    dve.wait_ge(S["sample_hi"], f + 1)
                    tt_(hxs[:, 1], hx[:, :, :], hxs[:, 0], ALU.subtract).then_inc(S["sample_lo"], 1)
                    dve.wait_ge(S["wt_hi"], f + 1)
                    stt_(wt[:, 1], p_wt, AS, wt[:, 0], ALU.mult, ALU.subtract).then_inc(S["wt_lo"], 1)
            def tile(f, it, i):
                e = it * 2 + i // K
                if i == 0:
                    dve.wait_ge(S["wb_done"], f * ITERS + it + 2)
                dve.wait_ge(S["up_mm"], f * 32 + it * 8 + (i + 1))
                dve.wait_ge(S["y_lo"], f * 32 + it * 8 + (i + FREE))
                dve.wait_ge(S["sig_done"], f * 32 + it * 8 + (i + 1))
                stt_(lin[:, i % 2], bank_up[i % 2][:, N:2 * N], b1s[:, bass.ds(e, 1), 1, i % K],
                     wb[:, i // K], ALU.add, ALU.mult)
                stt_(glu[:, i % 2], bank_up[i % 2][:, 0:N], b1s[:, bass.ds(e, 1), 0, i % K],
                     glu[:, i % 2], ALU.add, ALU.mult).then_inc(S["act_done"], 1)

            def moe_lo(it, c):
                per = HALF // CHUNK
                q = c // per
                at = (c % per) * CHUNK
                dve.wait_ge(S["moe_hi"], it * CONV + (c + 1))
                stt_(wm[:, 1, q % 2, 1, at:at + CHUNK], wm32[0][:, (q % 2) * HALF + at:(q % 2) * HALF + at + CHUNK],
                     WS, wm[:, 1, q % 2, 0, at:at + CHUNK], ALU.mult, ALU.subtract).then_inc(S["moe_lo"], 1)

            def l0_lo(q):
                dve.wait_ge(S["l0_hi"], q + 1)
                dst, src, hi = ((wbase[:, 1].rearrange("p k n -> p (k n)"), stage_l0[:, :],
                                 wbase[:, 0].rearrange("p k n -> p (k n)")),
                                (wla[:, 1].rearrange("p k n -> p (k n)"), st_la, wla[:, 0].rearrange("p k n -> p (k n)")),
                                (wlb[:, 1], st_lb, wlb[:, 0]))[q]
                stt_(dst, src, WS, hi, ALU.mult, ALU.subtract).then_inc(S["l0_split"], 1)

            def lap(it, visits):
                for s in range(LAP):
                    gru(it * LAP + s, it * LAP + s)
                    if visits == 2 and s % SPAN == 2:
                        x_lo(it * 2 + (2 + s // SPAN), s // SPAN % 2)
                    if visits == 1 and s in (10, 11, 12):
                        l0_lo(s - 10)
                    for c in range(CONV):
                        if c * LAP // CONV == s:
                            moe_lo(it, c)

            def blk(g, gru_on):
                f = g - 1
                if gru_on:
                    dve.wait_ge(S["gi_in"], g * 16)
                for s in range(HEAD):
                    if gru_on:
                        gru(g * TB + s, g % 2 * GIB + s)
                    head(s, f)
                with dve.Fori(0, ITERS) as it:
                    for s in range(STEPS):
                        if gru_on:
                            gru(g * TB + it * STEPS + (HEAD + s), g % 2 * GIB + it * STEPS + (HEAD + s))
                        if s == 0:
                            dve.wait_ge(S["act_done"], f * 32 + it * 8 + LEAD)
                            dve.wait_ge(S["wb_mm"], f * ITERS + it + 1)
                            ts_(wb[:, :, :], p_wb, YS / AS, None, ALU.mult).then_inc(S["wb_done"], 1)
                        for i in UPS[s]:
                            tile(f, it, i)
                dve.wait_ge(S["down_mm"], f * 32 + (32 + LEAD))
                for q in range(2):
                    v = x1[:, 2 * q:2 * q + 2, :].rearrange("p k n -> p (k n)")
                    stt_(v, bank_acc[q][:, :], 1 / PS, v, ALU.mult, ALU.add).then_inc(S["final_done"], 1)

            n = [0]

            def step(i):
                n[0] += 1
                i.then_inc(S["setup_dve"], 1)
                dve.wait_ge(S["setup_dve"], n[0])

            dve.wait_ge(S["bias_in"], 16 * 6)
            step(tt_(bi[:, 0:2 * K], bi[:, 0:2 * K], bh[:, 0:2 * K], ALU.add))
            step(ts_(bi[:, :], bi[:, :], PS, None, ALU.mult))
            for q in range(3):
                dve.wait_ge(S["wih_hi"], q + 1)
                stt_(part_of(wih[:, 1].rearrange("p k n -> p (k n)"), q), part_of(wm32[0], q), WS,
                     part_of(wih[:, 0].rearrange("p k n -> p (k n)"), q), ALU.mult, ALU.subtract
                     ).then_inc(S["wih_split"], 1)
                if q == 0:
                    x_lo(0, 0)
            step(ts_(bn[:, :, :], bh[:, 2 * K:3 * K].unsqueeze(2).to_broadcast([P, K, B]), PS, None, ALU.mult))
            step(ts_(b1sig[:, :, :], b1s[:, :, 0], 1.702, None, ALU.mult))
            step(ts_(b1s[:, :, 1], b1s[:, :, 1], 1.0, None, ALU.add))
            step(ts_(b1s[:, :, :, :], b1s[:, :, :, :], PS, None, ALU.mult))
            step(ts_(bg16[:, :], bg16[:, :], AS, None, ALU.mult))
            step(ts_(h[:, :, :], h[:, :, :], AS, None, ALU.mult))
            step(V.tensor_copy(hs[:, :, 0], h[:, :, :]))
            tt_(hs[:, :, 1], h[:, :, :], hs[:, :, 0], ALU.subtract).then_inc(S["h_ready"], 1)
            for q in range(3):
                dve.wait_ge(S["whh_hi"], q + 1)
                stt_(part_of(whh[:, 1].rearrange("p k n -> p (k n)"), q), part_of(wm32[1], q), WS,
                     part_of(whh[:, 0].rearrange("p k n -> p (k n)"), q), ALU.mult, ALU.subtract
                     ).then_inc(S["whh_split"], 1)
            x_lo(1, 1)
            dve.wait_ge(S["b2_hi"], 1)
            stt_(b2s[:, 1], b2f, WS, b2s[:, 0], ALU.mult, ALU.subtract).then_inc(S["b2_split"], 1)
            dve.wait_ge(S["gi_done"], G3)
            with dve.Fori(0, LAPS - 1) as it:
                lap(it, 2)
            lap(LAPS - 1, 1)
            dve.wait_ge(S["gi_done"], NB * G3)
            dve.wait_ge(S["const_in"], 16 * 6)
            with dve.Fori(1, NB) as g:
                blk(g, True)
            blk(NB, False)

        @block.gpsimd
        def _(pool):
            Q = nc.gpsimd

            def keep(t, col):
                pool.wait_ge(S["h_ready"], t + 2)
                apart(pool)
                dst = hf[:, :, :, col:col + 1] if isinstance(col, int) else hf[:, :, :, bass.ds(col, 1)]
                Q.tensor_copy(dst, h[:, :, :]).then_inc(S["h_kept"], 1)

            def grid_op(j, it):
                b = it * GRID_CHAIN + 1
                if j == 0:
                    pool.wait_ge(S["grid_in"], it * 16 + 16)
                else:
                    pool.wait_ge(S["grid_chain"], b + j)
                apart(pool)
                ts, tt, cp = Q.tensor_scalar, Q.tensor_tensor, Q.tensor_copy
                if j == 0:
                    i = ts(g_t, g_in, 1.0, 0.5 * (D - 1), ALU.add, ALU.mult)
                elif j == 1:
                    i = cp(g_int, g_t)
                elif j == 2:
                    i = cp(g_i0, g_int)
                elif j == 3:
                    i = tt(g_w1, g_i0, g_t, ALU.subtract)
                elif j == 4:
                    i = ts(g_w1, g_w1, 0.0, None, ALU.is_gt)
                elif j == 5:
                    i = tt(g_i0, g_i0, g_w1, ALU.subtract)
                elif j == 6:
                    i = tt(g_w1, g_t, g_i0, ALU.subtract)
                elif j == 7:
                    i = ts(g_w0, g_w1, -WS, WS, ALU.mult, ALU.add)
                elif j == 8:
                    i = ts(g_w1, g_w1, WS, None, ALU.mult)
                elif j == 9:
                    i = ts(g_i1, g_i0, -1.0, float(D - 2), ALU.max, ALU.min)
                elif j == 10:
                    i = ts(g_i0, g_i0, 0.0, float(D - 1), ALU.max, ALU.min)
                else:
                    k, o = (j - 11) // 7, (j - 11) % 7
                    hi, lo = gm[:, 0, bass.ds(it, 1), k], gm[:, 1, bass.ds(it, 1), k]
                    if o == 0:
                        i = ts(g_a, g_i0, iotf[:, k:k + 1], None, ALU.is_equal)
                    elif o == 1:
                        i = tt(g_a, g_a, g_w0, ALU.mult)
                    elif o == 2:
                        i = ts(g_t, g_i1, iotf[:, K + k:K + k + 1], None, ALU.is_equal)
                    elif o == 3:
                        i = tt(g_t, g_t, g_w1, ALU.mult)
                    elif o == 4:
                        i = tt(g_a, g_a, g_t, ALU.add)
                    elif o == 5:
                        i = cp(hi, g_a)
                    else:
                        i = tt(lo, g_a, hi, ALU.subtract)
                i.then_inc(S["grid_chain"], 1)

            def tile_y(f, it, i):
                pool.wait_ge(S["act_done"], f * 32 + it * 8 + (i + 1 + LEAD))
                Q.tensor_tensor(lin[:, i % 2], glu[:, i % 2], lin[:, i % 2], ALU.mult).then_inc(S["y_done"], 1)
                pool.wait_ge(S["y_hi"], f * 32 + it * 8 + (i + 1))
                Q.tensor_tensor(ys[:, i % 2, 1], lin[:, i % 2], ys[:, i % 2, 0], ALU.subtract).then_inc(S["y_lo"], 1)

            def lap(it):
                for s in range(LAP):
                    keep(it * LAP + s, it * LAP + s)
                    for j in range(GRID_CHAIN):
                        if j * LAP // GRID_CHAIN == s:
                            grid_op(j, it)

            def blk(g, gru_on):
                f = g - 1
                pool.wait_ge(S["h_kept"], f * TB + (TB + 1))
                pool.wait_ge(S["sample_lo"], f + 1)
                apart(pool)
                Q.tensor_copy(hx[:, K // 2:, :], hf_cols[:, K // 2:]).then_inc(S["hx_copied"], 1)
                if gru_on:
                    pool.wait_ge(S["hx_copied"], f + 1)
                    pool.wait_ge(S["h_lo"], f + 1)
                    apart(pool)
                for s in range(HEAD):
                    if gru_on:
                        keep(g * TB + s, s)
                with pool.Fori(0, ITERS) as it:
                    for s in range(STEPS):
                        if gru_on:
                            keep(g * TB + it * STEPS + (HEAD + s), it * STEPS + (HEAD + s))
                        for i in UPS[s]:
                            tile_y(f, it, i)

            for n in ("act_done", "y_done", "y_lo", "down_mm"):
                Q.sem_inc(S[n], LEAD)
            for n in ("grid_chain", "h_kept", "wb_done", "sample_lo"):
                Q.sem_inc(S[n], 1)
            Q.sem_inc(S["out_stored"], 16)
            for s in stored + gi_stored + [S["gi_in"]]:
                Q.sem_inc(s, 16)
            pool.wait_ge(S["const_in"], 16 * 6)
            pool.wait_ge(S["b2_split"], 1)
            pool.wait_ge(S["sel_ready"], 1)
            with pool.Fori(0, LAPS) as it:
                lap(it)
            pool.wait_ge(S["grid_chain"], LAPS * GRID_CHAIN + 1)
            with pool.Fori(1, NB) as g:
                blk(g, True)
            blk(NB, False)


def kernel(**inputs):
    import numpy as _np
    import concourse.bacc as _bacc
    from concourse import mybir as _mybir
    from concourse.bass_utils import run_bass_kernel_spmd as _run

    a = {k: _np.asarray(v) for k, v in inputs.items()}
    eye = _np.eye(P, dtype=_np.float32)

    def rows(w):
        return w.reshape(-1, P, w.shape[-1]).transpose(1, 0, 2)

    w1 = a["L1_ffn_w1"].reshape(E, D, 2, D).transpose(0, 3, 2, 1)
    w1 = w1.reshape(E, K, P, 2 * D).transpose(0, 2, 1, 3).reshape(E, P, 2 * K * D)
    w2 = a["L1_ffn_w2"].transpose(0, 2, 1).reshape(E, K, P, D).transpose(0, 2, 1, 3).reshape(E, P, K * D)
    moe = _np.concatenate([w1, w2], axis=2).reshape(E, P, 2, HALF).transpose(0, 2, 1, 3).reshape(2 * E, P, HALF)
    b1 = a["L1_ffn_b1"].reshape(E, K, P, 2).transpose(2, 0, 3, 1)
    arrays = {
        "x": a["x"].reshape(B, NB, TB, K, P).transpose(1, 4, 3, 0, 2).reshape(NB, P, K, N),
        "h0": a["cond_2048"].reshape(B, K, P).transpose(2, 1, 0),
        "grid": a["cond_2048"],
        "w_ih": rows(a["L0_cond_W_ih"]).reshape(P, -1),
        "w_hh": rows(a["L0_cond_W_hh"]).reshape(P, -1),
        "b_ih": a["L0_cond_b_ih"].reshape(G3, P).T,
        "b_hh": a["L0_cond_b_hh"].reshape(G3, P).T,
        "w_base": rows(a["L0_ffn_weight"].T).reshape(P, -1),
        "lora_a": rows(a["L0_ffn_lora_A"].reshape(E * RANK, D).T).reshape(P, -1),
        "lora_b": a["L0_ffn_lora_B"].transpose(0, 2, 1).reshape(E * RANK, D),
        "w_router": rows(a["L0_ffn_router_w"].T),
        "w_gate": rows(a["L1_ffn_gate_w"].T),
        "b_gate": a["L1_ffn_gate_b"].reshape(1, E),
        "w_moe": moe,
        "b1": b1,
        "b2": a["L1_ffn_b2"],
        "ident": eye,
        "sel_all": _np.repeat(eye[:E, :E], P, axis=1).reshape(E, E, P),
        "iota_e": _np.broadcast_to(_np.arange(E, dtype=_np.float32), (P, E)),
        "iota_f": (_np.arange(2 * D, dtype=_np.float32) % D - _np.repeat([0, 1], D)).astype(_np.float32).reshape(2 * K, P).T,
    }
    arrays = {k: _np.ascontiguousarray(v) for k, v in arrays.items()}
    nc = _bacc.Bacc("TRN2", target_bir_lowering=False, num_devices=1, dynamic_dma_scratch_size=2048)
    args = [nc.dram_tensor(f"in_{k}", v.shape, _mybir.dt.from_np(v.dtype), kind="ExternalInput").ap()
            for k, v in arrays.items()]
    out = nc.dram_tensor("out", (NB, P, K, N), F32, kind="ExternalOutput").ap()
    adaln_ffn_kernel(nc, *args, out)
    r = _run(nc, [{f"in_{k}": v for k, v in arrays.items()}], core_ids=[0])
    got = _np.asarray(r.results[0]["out"])
    return _np.ascontiguousarray(got.reshape(NB, P, K, B, TB).transpose(3, 0, 4, 2, 1).reshape(B, T, D))
```
